# Optimizing a Trainium2 kernel written in Bass

```python
import numpy as np
import jax
import jax.numpy as jnp

def _softmax(x, axis=-1):
    return jax.nn.softmax(x, axis=axis)

def _gelu(x):
    return jax.nn.gelu(x, approximate=True)

def _silu(x):
    return jax.nn.silu(x)

def _sigmoid(x):
    return jax.nn.sigmoid(x)

def _layernorm(x, axis=-1, eps=1e-05):
    m = jnp.mean(x, axis=axis, keepdims=True)
    v = jnp.var(x, axis=axis, keepdims=True)
    return (x - m) / jnp.sqrt(v + eps)

def _scatter_add(tgt, idx, src, axis=0):
    return tgt.at[idx].add(src)

def _segment_sum(src, seg, n):
    return jax.ops.segment_sum(src, seg, n)
kernel_name = 'mk_cond_resid_d1_seqx_r2_e45556'

def setup_inputs(seed: int=0):
    np.random.seed(seed)
    _w = jnp.asarray

    def _rec_inputs():
        import jax
        import jax.numpy as jnp
        _rk = jax.random.key(seed)
        x = -0.0003929 + 0.9999 * jax.random.normal(jax.random.fold_in(_rk, 1), (4, 1024, 512), jnp.float32)
        _lenS = 1024 - jax.random.randint(jax.random.fold_in(_rk, 7), (4,), 0, max(1, 1024 // 4) + 1, jnp.int32)
        _lenS2 = 1024 - jax.random.randint(jax.random.fold_in(_rk, 8), (4,), 0, max(1, 1024 // 4) + 1, jnp.int32)
        cond_2048 = 0.00782532 + 1.00527 * jax.random.normal(jax.random.fold_in(_rk, 11), (4, 1024), jnp.float32)
        return (x, cond_2048)
    x, cond_2048 = _rec_inputs()

    def _L0_cond_setup():
        import jax, jax.numpy as jnp
        import numpy as np
        B, S, D_MODEL, D_INNER, D_STATE = (4, 2048, 512, 1024, 16)
        key = jax.random.key(seed)
        ks = jax.random.split(key, 12)
        inp = {'x': jax.random.normal(ks[0], (B, S, D_MODEL), jnp.float32), 't_emb': jax.random.normal(ks[1], (B, D_INNER), jnp.float32), 'W_in': jax.random.normal(ks[2], (2 * D_INNER, D_MODEL), jnp.float32) * 0.02, 'W_conv': jax.random.normal(ks[3], (D_INNER, 1, 4), jnp.float32) * 0.1, 'b_conv': jnp.zeros((D_INNER,), jnp.float32), 'ln_g': jnp.ones((D_INNER,), jnp.float32), 'ln_b': jnp.zeros((D_INNER,), jnp.float32), 'W_xproj': jax.random.normal(ks[4], (3 * D_STATE, D_INNER), jnp.float32) * 0.02, 'W_dt': jax.random.normal(ks[5], (D_STATE, D_STATE), jnp.float32) * 0.01, 'b_dt': jax.random.uniform(ks[6], (D_STATE,), jnp.float32) * 0.1, 'A_log': jax.random.normal(ks[7], (D_STATE,), jnp.float32) * 0.1, 'D': jnp.ones((D_INNER,), jnp.float32) * 0.1, 'W_out': jax.random.normal(ks[8], (D_MODEL, D_INNER), jnp.float32) * 0.02}
        return inp
    _L0_cond_all = _L0_cond_setup()
    _L0_cond_in = {k: v for k, v in _L0_cond_all.items() if k in ('W_in', 'W_conv', 'b_conv', 'ln_g', 'ln_b', 'W_xproj', 'W_dt', 'b_dt', 'A_log', 'D', 'W_out')}
    del _L0_cond_all
    return {'x': x, 'cond_2048': cond_2048, 'L0_cond_W_in': _L0_cond_in['W_in'], 'L0_cond_W_conv': _L0_cond_in['W_conv'], 'L0_cond_b_conv': _L0_cond_in['b_conv'], 'L0_cond_ln_g': _L0_cond_in['ln_g'], 'L0_cond_ln_b': _L0_cond_in['ln_b'], 'L0_cond_W_xproj': _L0_cond_in['W_xproj'], 'L0_cond_W_dt': _L0_cond_in['W_dt'], 'L0_cond_b_dt': _L0_cond_in['b_dt'], 'L0_cond_A_log': _L0_cond_in['A_log'], 'L0_cond_D': _L0_cond_in['D'], 'L0_cond_W_out': _L0_cond_in['W_out']}

def reference(x, cond_2048, L0_cond_W_in, L0_cond_W_conv, L0_cond_b_conv, L0_cond_ln_g, L0_cond_ln_b, L0_cond_W_xproj, L0_cond_W_dt, L0_cond_b_dt, L0_cond_A_log, L0_cond_D, L0_cond_W_out):
    import jax
    import jax.numpy as jnp

    def _L0_cond_ref(x, t_emb, W_in, W_conv, b_conv, ln_g, ln_b, W_xproj, W_dt, b_dt, A_log, D, W_out):
        import jax, jax.numpy as jnp
        import numpy as np
        B, S, D_MODEL, D_INNER, D_STATE = (4, 2048, 512, 1024, 16)
        d_inner = W_conv.shape[0]
        d_state = A_log.shape[0]
        xr, gate = jnp.split(x @ W_in.T, 2, axis=-1)
        xr = xr + t_emb[:, None, :]
        xc = jax.lax.conv_general_dilated(xr.transpose(0, 2, 1), W_conv, (1,), [(3, 0)], feature_group_count=d_inner, dimension_numbers=('NCH', 'OIH', 'NCH')) + b_conv[None, :, None]
        xc = jax.nn.silu(xc).transpose(0, 2, 1)
        mu = xc.mean(-1, keepdims=True)
        var = xc.var(-1, keepdims=True)
        xn = (xc - mu) / jnp.sqrt(var + 1e-05) * ln_g + ln_b
        Bm, Cm, dt = jnp.split(xn @ W_xproj.T, 3, axis=-1)
        dt = jnp.tanh(dt @ W_dt.T + b_dt) * 0.01
        A = -jnp.tanh(A_log)
        Ad = 1.0 + dt * A
        Bd = Bm * jnp.minimum(jnp.linalg.norm(xn, axis=-1, keepdims=True), 1.0)
        h0 = jnp.zeros((xn.shape[0], d_state, d_inner), xn.dtype)

        def step(h, inputs):
            ad, bd, xt, ct = inputs
            h = jnp.clip(h * ad[:, :, None] + bd[:, :, None] * xt[:, None, :], -10.0, 10.0)
            yt = jnp.einsum('bd,bdh->bh', ct, h)
            return (h, yt)
        _, ys = jax.lax.scan(step, h0, (Ad.transpose(1, 0, 2), Bd.transpose(1, 0, 2), xn.transpose(1, 0, 2), Cm.transpose(1, 0, 2)))
        y = ys.transpose(1, 0, 2) + D * xn
        return y * jax.nn.silu(gate) @ W_out.T
    x = x + _L0_cond_ref(x, cond_2048, L0_cond_W_in, L0_cond_W_conv, L0_cond_b_conv, L0_cond_ln_g, L0_cond_ln_b, L0_cond_W_xproj, L0_cond_W_dt, L0_cond_b_dt, L0_cond_A_log, L0_cond_D, L0_cond_W_out)
    return x

_drawn_inputs = setup_inputs


def setup_inputs(seed=0):
    import zlib

    import numpy as np

    out = dict(_drawn_inputs(seed))
    spreads = {'L0_cond_b_conv': (0.0, 0.1),
     'L0_cond_ln_g': (1.0, 0.2),
     'L0_cond_ln_b': (0.0, 0.1),
     'L0_cond_D': (0.10000000149011612, 0.6)}
    factors = {'L0_cond_W_dt': 8.0, 'L0_cond_b_dt': 8.0, 'L0_cond_A_log': 8.0}
    for name, (base, spread) in spreads.items():
        noise = np.random.default_rng([zlib.crc32(name.encode()), seed]).standard_normal(out[name].shape)
        drawn = base * np.exp(spread * noise) if base else spread * noise
        out[name] = jnp.asarray(drawn.astype(out[name].dtype))
    for name, factor in factors.items():
        out[name] = (out[name] * factor).astype(out[name].dtype)
    return out
```

```python
from contextlib import ExitStack

import concourse.bass as bass
from concourse import mybir

F32 = mybir.dt.float32
BF16 = mybir.dt.bfloat16
ALU = mybir.AluOpType
ACT = mybir.ActivationFunctionType

P = 128
B, S, DM, DI, NS = 4, 1024, 512, 1024, 16
TAPS = 4
T = 32
NCH = S // T
TOK = B * T
NT = DI // P
KC = DM // P
HALF = DI // 2
GRP = 16
NG = T // GRP
SLOTS = T // 4
RING = 8
XB = 4
SPLIT = 3
XROWS = 2 * SPLIT
XK = XROWS * 4 * B
PRM_DMAS = 2 * B
EPS = 1e-5
LIM = 10.0
HIST = TAPS - 1
DMA = 16

GATE1, STATS, PROJ, TOK0, TOK1, XT, XR0, XR1, GATE0 = range(9)
V_BCONV, V_G, V_B, V_D, V_TEMB, V_ALL = TAPS, TAPS + 1, TAPS + 2, TAPS + 3, TAPS + 4, TAPS + 4 + B


def job(k, place):
    if isinstance(k, int):
        if k == -2:
            return place - XT
        if k == NCH - 2 and place > XR1:
            return 9 * k + 11 + place - 3
        if k == NCH - 1:
            return 9 * k + 11 + place - 3
    return k * 9 + (11 + place)


def job_bank(k, par, place):
    return job(k, place) % 2 if isinstance(k, int) else (par + 1 + place) % 2


def build(nc, x, vec, w_in, w_out, w_bc, w_dtx, w_dt, nvec, sel, ident, perm, mask, out):
    with ExitStack() as ctx:
        def sb(name, shape, dt=F32):
            return ctx.enter_context(nc.sbuf_tensor(name, shape, dt))

        def ps(name):
            return ctx.enter_context(nc.psum_tensor(name, [P, 512], F32))

        def sem(name):
            return ctx.enter_context(nc.semaphore(name))

        w_in_s = sb("w_in_s", [P, KC, 2 * DI])
        w_out_s = sb("w_out_s", [P, NT, DM])
        w_proj = sb("w_proj", [P, NT, 32, 3])
        w_dtx_s = sb("w_dtx_s", [NS, NT, P])
        w_dt_s = sb("w_dt_s", [NS, 32])
        vec_s = sb("vec_s", [P, NT, V_ALL])
        nvec_s = sb("nvec_s", [P, 2])
        neg_a = sb("neg_a", [P, 2])
        sel_s = sb("sel_s", [XK, 4, P], BF16)
        ident_s = sb("ident_s", [P, P])
        perm_s = sb("perm_s", [P, P])
        mask_s = sb("mask_s", [P, 8])
        mean_w = sb("mean_w", [P, P])
        ones_w = sb("ones_w", [P, 32])
        zeros = sb("zeros", [P, T])
        conv_bias = sb("conv_bias", [P, NT, B])
        neg_w = sb("neg_w", [P, NT, TAPS])
        w_sum = sb("w_sum", [P, NT, 2])
        x_in = sb("x_in", [P, DM])
        x_t = sb("x_t", [P, 2, KC, TOK])
        taps = [sb(f"taps{q}", [P, 4, TAPS, B, HIST + T]) for q in range(2)]
        cv = [sb(f"cv{q}", [P, 512]) for q in range(2)]
        cv2 = sb("cv2", [P, 512])
        xn = sb("xn", [P, NT, TOK])
        sq = sb("sq", [P, NT, TOK])
        st = sb("st", [P, 3, TOK])
        rs = sb("rs", [P, 3, TOK])
        d_xn = [sb(f"d_xn{i}", [P, NT, TOK]) for i in range(2)]
        gate = [sb(f"gate{i}", [P, NT, TOK]) for i in range(2)]
        pr = sb("pr", [P, TOK])
        x_tok = [sb(f"x_tok{h}", [P, 512]) for h in range(2)]
        rem = sb("rem", [P, 512])
        parts = [sb(f"parts{h}", [P, SPLIT, 512], BF16) for h in range(2)]
        xs = [sb(f"xs{i}", [XK, T // 4, 512], BF16) for i in range(2)]
        prm = sb("prm", [P, 4, T])
        tmp = sb("tmp", [P, 4, T])
        prod = sb("prod", [P, 2, T])
        inv = sb("inv", [P, T])
        cp = sb("cp", [P, T])
        par = [sb(f"par{i}", [P, 3, T]) for i in range(2)]
        cw = [sb(f"cw{g}", [P, 4 * (4 * 32 + 8)]) for g in range(NG)]
        w = sb("w", [P, 512])
        g = sb("g", [P, RING, 512])
        y_row = [sb(f"y_row{i}", [P, 512]) for i in range(2)]
        y_sum = [sb(f"y_sum{i}", [P, 32, GRP]) for i in range(2)]
        yg = [sb(f"yg{i}", [P, NT * B, T]) for i in range(2)]
        x_res = sb("x_res", [P, DM])
        o_sb = [sb(f"o_sb{i}", [P, DM]) for i in range(2)]

        xb = [ps(f"xb{i}") for i in range(XB)]
        y_ps = ps("y_ps")
        a_ps = [ps(f"a_ps{i}") for i in range(2)]
        b_ps = ps("b_ps")

        w_loaded, ready0 = sem("w_loaded"), sem("ready0")
        x_loaded, res_loaded, prm_loaded, xs_loaded, stored = (
            sem(n) for n in ("x_loaded", "res_loaded", "prm_loaded", "xs_loaded", "stored"))
        a_full, a_free, b_full, b_free = (sem(n) for n in ("a_full", "a_free", "b_full", "b_free"))
        xt_ready, taps_ready, taps_free, conv_done, silu_done, sq_done = (
            sem(n) for n in ("xt_ready", "taps_ready", "taps_free", "conv_done", "silu_done", "sq_done"))
        st_ready, ln_step, ln_done, xn_ready, sq_n_done, dxn_ready, gate_ready = (
            sem(n) for n in ("st_ready", "ln_step", "ln_done", "xn_ready", "sq_n_done", "dxn_ready", "gate_ready"))
        pr_ready, tok_ready, hi_ready, rem_ready, mid_ready, lo_ready = (
            sem(n) for n in ("pr_ready", "tok_ready", "hi_ready", "rem_ready", "mid_ready", "lo_ready"))
        th_ready, a_ready, prod_ready, inv_ready, par_ready, cp_ready, cw_ready, pool_step = (
            sem(n) for n in ("th_ready", "a_ready", "prod_ready", "inv_ready", "par_ready", "cp_ready", "cw_ready", "pool_step"))
        x_bc, x_used, clipped, y_batch, y_rows, y_summed, gated, out_ready = (
            sem(n) for n in ("x_bc", "x_used", "clipped", "y_batch", "y_rows", "y_summed", "gated", "out_ready"))
        conv_step, dve0, act0, pe0 = sem("conv_step"), sem("dve0"), sem("act0"), sem("pe0")
        bn_ready, u_ready, var_ready, std_ready, rstd_ready = (sem(n) for n in ("bn_ready", "u_ready", "var_ready", "std_ready", "rstd_ready"))

        def chan(jh):
            return (jh % 2) * HALF + (jh // 2) * P

        def chunks(eng, one):
            first = 3
            for k in range(-2, first):
                one(k, k % 2)
            turns = (NCH - 3 - first) // 2
            with eng.Fori(0, turns) as i:
                one(i * 2 + first, first % 2)
                one(i * 2 + (first + 1), (first + 1) % 2)
            for k in range(first + 2 * turns, NCH + 1):
                one(k, k % 2)

        def has(k, lo, hi):
            return lo <= k <= hi if isinstance(k, int) else True

        block = ctx.enter_context(nc.Block())

        @block.sync
        def _(sp):
            for dst, src in ((x_in[:, :], x[:, 0:T, :]), (w_in_s[:, :, 0:DI], w_in.rearrange("(c p) n -> p c n", p=P)[:, :, 0:DI]),
                             (vec_s[:, :, :], vec), (ident_s[:, :], ident), (w_proj[:, :, :, :], w_bc),
                             (w_dtx_s[:, :, :], w_dtx), (w_dt_s[:, :], w_dt), (nvec_s[:, :], nvec),
                             (sel_s[:, :, :], sel), (perm_s[:, :], perm), (mask_s[:, :], mask),
                             (w_in_s[:, :, DI:2 * DI], w_in.rearrange("(c p) n -> p c n", p=P)[:, :, DI:2 * DI]),
                             (w_out_s[:, :, :], w_out)):
                d = sp.dma_start(dst, src)
                d.then_inc(x_loaded if dst.tensor.name == x_in.name else w_loaded, DMA)

            def one(k, kp):
                np_ = (kp + 1) % 2

                def val(v):
                    return v if isinstance(v, int) else sp.snap(v)

                k0, k1, k2, steps = val(k), val(k + 1), val(k + 2), val(k * T)
                lo_h = [val(k * 2 + (3 + h)) for h in range(2)]
                turned = val(job(k, XT) + 1)
                at_prev, at_this, at_next = val((k - 1) * T), val(k * T), val((k + 3) * T)
                if has(k, 1, NCH):
                    sp.wait_ge(out_ready, k0)
                    sp.dma_start(out[:, bass.ds(at_prev, T), :], o_sb[np_][:, :]).then_inc(stored, DMA)
                if has(k, 0, NCH - 1):
                    if has(k, 0, NCH - 2):
                        sp.wait_ge(par_ready, k1)
                        sp.wait_ge(cp_ready, k1)
                    sp.dma_start(x_res[:, :], x[:, bass.ds(at_this, T), :]).then_inc(res_loaded, DMA)
                if has(k, -1, NCH - 2):
                    sp.wait_ge(pr_ready, k2)
                    for b in range(B):
                        sp.dma_start(prm[32 * b:32 * b + 32, 0:3, :], pr[0:96, T * b:T * b + T]).then_inc(prm_loaded, DMA)
                        sp.dma_start(prm[32 * b:32 * b + 32, 3, :], pr[96:P, T * b:T * b + T]).then_inc(prm_loaded, DMA)
                    if has(k, 1, NCH):
                        sp.wait_ge(x_bc, steps)
                    for h in range(2):
                        sp.wait_ge(lo_ready, lo_h[h])
                        wide = xs[np_][:, :, :].ap[0][0]
                        for part in range(SPLIT):
                            rows = bass.AP(tensor=xs[np_][:, :, :].tensor, offset=(2 * part + h) * wide,
                                           ap=[[XROWS * wide, 4 * B], [512, T // 4], [1, 512]])
                            sp.dma_start(rows, parts[h][:, part, :]).then_inc(xs_loaded, DMA)
                if has(k, -2, NCH - 4):
                    sp.wait_ge(a_full, turned)
                    sp.dma_start(x_in[:, :], x[:, bass.ds(at_next, T), :]).then_inc(x_loaded, DMA)

            chunks(sp, one)
            sp.wait_ge(stored, DMA * NCH)

        @block.tensor
        def _(pe):
            def open_job(k, place):
                n = job(k, place)
                if not isinstance(n, int) or n >= 2:
                    pe.wait_ge(a_free, n - 1)

            def in_quad(k, kp, chunk_par, place, quad, col0, s):
                if s == 0:
                    open_job(k, place)
                jh = 4 * quad + s
                for c in range(KC):
                    mm = pe.matmul(a_ps[job_bank(k, kp, place)][:, TOK * s:TOK * s + TOK],
                                   w_in_s[:, c, col0 + chan(jh):col0 + chan(jh) + P],
                                   x_t[:, chunk_par, c, :], start=(c == 0), stop=(c == KC - 1))
                if s == 3:
                    mm.then_inc(a_full, 1)

            def x_transpose(k, kp):
                open_job(k, XT)
                pe.wait_ge(x_loaded, (k + 3) * DMA)
                for c in range(KC):
                    mm = pe.transpose(a_ps[job_bank(k, kp, XT)][:, TOK * c:TOK * c + TOK],
                                      x_in[:, P * c:P * c + P], ident_s[:, :])
                mm.then_inc(a_full, 1)

            def bring_x(k, kp, t):
                q = t // (T // 4)
                if isinstance(k, int) and k == 0 and t < XB:
                    pass
                else:
                    pe.wait_ge(x_used, k * T + (t - XB + 1))
                pe.matmul(xb[t % XB][:, :], sel_s[:, q, :], xs[kp][:, t % (T // 4), :],
                          start=True, stop=True).then_inc(x_bc, 1)

            def contract(k, slot):
                grp, r = slot // 4, slot % 4
                pe.wait_ge(clipped, k * T + 4 * slot + 4)
                if r == 0:
                    if grp == 0:
                        pe.wait_ge(cw_ready, k * 2 + 1)
                    else:
                        pe.wait_ge(cw_ready, k * 2 + 2)
                    if not (isinstance(k, int) and k == 0 and grp == 0):
                        pe.wait_ge(y_rows, k * 2 + grp)
                for c in range(4):
                    t = 4 * slot + c
                    s = 4 * r + c
                    mm = pe.matmul(y_ps[32 * c:32 * c + 32, :], cw[grp][:, 32 * s:32 * s + 32], g[:, t % RING, :],
                                   start=(r == 0), stop=(r == 3), tile_position=(0, 32 * c))
                mm.then_inc(y_batch, 1)

            def y_turn(k, grp):
                pe.wait_ge(y_rows, k * 2 + (grp + 1))
                n = k * 3 + (0 if grp == 0 else 1)
                if not (isinstance(n, int) and n == 0):
                    pe.wait_ge(b_free, n)
                for j in range(4):
                    mm = pe.transpose(b_ps[:, P * j:P * j + P], y_row[grp][:, P * j:P * j + P], perm_s[:, :])
                mm.then_inc(b_full, 1)

            def out_part(k, kp, quarter):
                if quarter == 0:
                    pe.wait_ge(gated, k * 2 + 2)
                    pe.wait_ge(b_free, k * 3 + 2)
                    if isinstance(k, int) and k == 0:
                        pe.wait_ge(w_loaded, 12 * DMA)
                jh = quarter
                mm = pe.matmul(b_ps[:, :], yg[kp][:, B * jh:B * jh + B, :], w_out_s[:, jh, :],
                               start=(jh == 0), stop=(jh == NT - 1))
                if jh == NT - 1:
                    mm.then_inc(b_full, 1)

            def stats(k, kp, part):
                if part == 0:
                    open_job(k, STATS)
                    pe.wait_ge(silu_done, k * 2 + 4)
                else:
                    pe.wait_ge(sq_done, k * 2 + 4)
                src = (xn, sq)[part]
                for jh in range(NT):
                    mm = pe.matmul(a_ps[job_bank(k, kp, STATS)][:, TOK * part:TOK * part + TOK], mean_w[:, :], src[:, jh, :],
                                   start=(jh == 0), stop=(jh == NT - 1))
                if part == 1:
                    mm.then_inc(a_full, 1)

            def project(k, kp, part):
                if part == 0:
                    open_job(k, PROJ)
                    pe.wait_ge(xn_ready, k + 2)
                    pe.wait_ge(sq_n_done, k + 2)
                for jh in range(4 * part, 4 * part + 4):
                    for kind in range(4):
                        lhs = w_cols[:, jh, 32 * kind:32 * kind + 32] if kind < 3 else ones_w[:, :]
                        mm = pe.matmul(a_ps[job_bank(k, kp, PROJ)][32 * kind:32 * kind + 32, 0:TOK], lhs,
                                       (xn if kind < 3 else sq)[:, jh, :], start=(jh == 0), stop=(jh == NT - 1),
                                       tile_position=(0, 32 * kind))
                if part == 1:
                    mm.then_inc(a_full, 1)

            w_cols = w_proj[:, :, :, :].rearrange("p a s k -> p a (s k)")

            def to_tokens(k, kp, h):
                place = (TOK0, TOK1)[h]
                open_job(k, place)
                for j in range(4):
                    mm = pe.transpose(a_ps[job_bank(k, kp, place)][:, P * j:P * j + P], xn[:, 2 * j + h, :], ident_s[:, :])
                mm.then_inc(a_full, 1)

            pe.wait_ge(w_loaded, 12 * DMA)
            pe.wait_ge(ready0, 2)
            for jh in range(NT):
                mm = pe.matmul(b_ps[:, 32 * jh:32 * jh + 32], w_dtx_s[:, jh, :], w_dt_s[:, :], start=True, stop=True)
            mm.then_inc(pe0, 1)
            pe.wait_ge(dve0, 1)

            def one(k, kp):
                np_ = (kp + 1) % 2
                scan, front1, front2 = has(k, 0, NCH - 1), has(k, -2, NCH - 3), has(k, -1, NCH - 2)
                back = has(k, 1, NCH)
                for slot in range(SLOTS):
                    for s in range(4):
                        t = 4 * slot + s
                        if scan:
                            if t == 0 and isinstance(k, int) and k == 0:
                                pe.wait_ge(xs_loaded, 2 * SPLIT * DMA)
                                for first in range(XB - 1):
                                    bring_x(k, kp, first)
                            if t + XB - 1 < T:
                                bring_x(k, kp, t + XB - 1)
                            elif has(k, 0, NCH - 2):
                                if t + XB - 1 == T:
                                    pe.wait_ge(xs_loaded, (k + 2) * (2 * SPLIT * DMA))
                                bring_x(k + 1, np_, t + XB - 1 - T)
                        if s == 1:
                            if slot == 0 and back:
                                contract(k - 1, SLOTS - 1)
                            if slot > 0 and scan:
                                contract(k, slot - 1)
                        if slot == 0 and scan:
                            if s == 0:
                                pe.wait_ge(xt_ready, k + 1)
                            in_quad(k, kp, kp, GATE1, 1, DI, s)
                        if slot == 1 and s == 0 and back:
                            y_turn(k - 1, 1)
                        if slot == 1 and s in (1, 3) and front2:
                            stats(k, kp, s // 2)
                        if slot in (2, 3) and back:
                            out_part(k - 1, np_, 4 * (slot - 2) + s)
                        if slot == 4 and s < 2 and front2:
                            project(k, kp, s)
                        if slot == 4 and s == 2 and front2:
                            to_tokens(k, kp, 0)
                            to_tokens(k, kp, 1)
                        if slot == 4 and s == 3 and front1:
                            x_transpose(k, kp)
                        if slot == 5 and s == 0 and scan:
                            y_turn(k, 0)
                        if slot == 5 and front1:
                            if s == 0:
                                pe.wait_ge(xt_ready, k + 3)
                            in_quad(k, kp, kp, XR0, 0, 0, s)
                        if slot == 6 and front1:
                            in_quad(k, kp, kp, XR1, 1, 0, s)
                        if slot == 7 and front2:
                            in_quad(k, kp, np_, GATE0, 0, DI, s)

            chunks(pe, one)

        @block.scalar
        def _(act):
            def take(k, kp, place):
                act.wait_ge(a_full, job(k, place) + 1)
                return a_ps[job_bank(k, kp, place)]

            act.wait_ge(w_loaded, 12 * DMA)
            act.activation(neg_a[:, 0:1], nvec_s[:, 0:1], ACT.Tanh).then_inc(act0, 1)
            act.wait_ge(act0, 1)
            act.activation(neg_a[:, 1:2], neg_a[:, 0:1], ACT.Copy, scale=-0.01).then_inc(act0, 1)
            act.wait_ge(act0, 2)
            act.wait_ge(dve0, 2)

            def gates(k, kp, place, quad, chunk_par):
                src = take(k, kp, place)
                act.activation(gate[chunk_par][:, 4 * quad:4 * quad + 4, :].rearrange("p a b -> p (a b)"), src[:, :],
                               ACT.Silu).then_inc(a_free, 1)

            def rows_out(k, grp):
                act.wait_ge(y_batch, k * SLOTS + 4 * (grp + 1))
                if has(k, 1, NCH):
                    act.wait_ge(b_full, k * 3 - (2 if grp == 0 else 1))
                act.activation(y_row[grp][:, :], y_ps[:, :], ACT.Copy).then_inc(y_rows, 1)

            def silu(c, quad):
                act.wait_ge(conv_done, c * 2 + (quad + 1))
                part = xn[:, 4 * quad:4 * quad + 4, :].rearrange("p a b -> p (a b)")
                act.activation(part, cv[quad][:, :], ACT.Silu).then_inc(silu_done, 1)
                act.wait_ge(silu_done, c * 2 + (quad + 1))
                act.activation(sq[:, 4 * quad:4 * quad + 4, :].rearrange("p a b -> p (a b)"), part,
                               ACT.Square).then_inc(sq_done, 1)

            def tap_products(k, kp, quad):
                src = take(k, kp, (XR0, XR1)[quad])
                act.wait_ge(taps_free, k * 2 + (4 + quad + 1))
                for d in range(4):
                    for tap in range(TAPS):
                        last = act.activation(taps[quad][:, d, tap, :, HIST:HIST + T],
                                              src[:, TOK * d:TOK * d + TOK].rearrange("p (b t) -> p b t", b=B),
                                              ACT.Copy, scale=vec_s[:, 4 * quad + d, tap:tap + 1])
                last.then_inc(a_free, 1)

            def one(k, kp):
                np_ = (kp + 1) % 2
                scan, front1, front2 = has(k, 0, NCH - 1), has(k, -2, NCH - 3), has(k, -1, NCH - 2)
                back = has(k, 1, NCH)
                if scan:
                    gates(k, kp, GATE1, 1, kp)
                if back:
                    rows_out(k - 1, 1)
                if front2:
                    silu(k + 1, 1)
                    src = take(k, kp, STATS)
                    act.activation(st[:, 0, :], src[:, 0:TOK], ACT.Copy)
                    act.activation(st[:, 1, :], src[:, 0:TOK], ACT.Square)
                    act.activation(st[:, 2, :], src[:, TOK:2 * TOK], ACT.Copy, bias=EPS).then_inc(a_free, 1)
                    act.wait_ge(var_ready, k + 2)
                    act.activation(rs[:, 1, :], rs[:, 0, :], ACT.Sqrt).then_inc(std_ready, 1)
                    for jh in range(NT):
                        if jh % 4 == 0:
                            act.wait_ge(ln_done, k * 2 + (3 + jh // 4))
                        last = act.activation(xn[:, jh, :], xn[:, jh, :], ACT.Identity, bias=vec_s[:, jh, V_B:V_B + 1],
                                              scale=vec_s[:, jh, V_G:V_G + 1])
                    last.then_inc(xn_ready, 1)
                    act.wait_ge(xn_ready, k + 2)
                    act.activation(sq[:, :, :].rearrange("p a b -> p (a b)"), xn[:, :, :].rearrange("p a b -> p (a b)"),
                                   ACT.Square).then_inc(sq_n_done, 1)
                    if has(k, 1, NCH):
                        act.wait_ge(y_summed, k * 2)
                    for jh in range(NT):
                        last = act.activation(d_xn[np_][:, jh, :], xn[:, jh, :], ACT.Copy, scale=vec_s[:, jh, V_D:V_D + 1])
                    last.then_inc(dxn_ready, 1)
                if scan:
                    rows_out(k, 0)
                if front2:
                    src = take(k, kp, PROJ)
                    if has(k, 0, NCH):
                        act.wait_ge(prm_loaded, (k + 1) * (PRM_DMAS * DMA))
                    act.activation(pr[:, :], src[:, 0:TOK], ACT.Copy).then_inc(pr_ready, 1)
                    act.wait_ge(pr_ready, k + 2)
                    act.sem_inc(a_free, 1)
                    for h in range(2):
                        src = take(k, kp, (TOK0, TOK1)[h])
                        if has(k, 0, NCH):
                            act.wait_ge(lo_ready, k * 2 + (h + 1))
                            act.wait_ge(xs_loaded, (k + 1) * (2 * SPLIT * DMA))
                        act.activation(x_tok[h][:, :], src[:, :], ACT.Copy).then_inc(tok_ready, 1)
                        act.activation(parts[h][:, 0, :], src[:, :], ACT.Copy).then_inc(hi_ready, 1)
                        act.wait_ge(hi_ready, k * 2 + (3 + h))
                        act.wait_ge(tok_ready, k * 2 + (3 + h))
                        act.sem_inc(a_free, 1)
                if front1:
                    src = take(k, kp, XT)
                    act.activation(x_t[:, kp, :, :].rearrange("p a b -> p (a b)"), src[:, :], ACT.Copy).then_inc(xt_ready, 1)
                    act.wait_ge(xt_ready, k + 3)
                    act.sem_inc(a_free, 1)
                if front2:
                    for h in range(2):
                        act.wait_ge(rem_ready, k * 2 + (3 + h))
                        act.activation(parts[h][:, 1, :], x_tok[h][:, :], ACT.Copy).then_inc(mid_ready, 1)
                if front1:
                    tap_products(k, kp, 0)
                if front2:
                    act.wait_ge(prm_loaded, (k + 2) * (PRM_DMAS * DMA))
                    act.activation(tmp[:, 2, :], prm[:, 2, :], ACT.Tanh, bias=nvec_s[:, 1:2]).then_inc(th_ready, 1)
                    act.wait_ge(th_ready, k + 2)
                    act.activation(tmp[:, 3, :], tmp[:, 2, :], ACT.Copy, scale=neg_a[:, 1:2], bias=1.0).then_inc(a_ready, 1)
                    act.activation(tmp[:, 1, :], prm[:, 3, :], ACT.Sqrt).then_inc(bn_ready, 1)
                if front1:
                    tap_products(k, kp, 1)
                    silu(k + 2, 0)
                if front2:
                    gates(k, kp, GATE0, 0, np_)

            chunks(act, one)

        @block.vector
        def _(dve):
            dve.memset(mean_w[:, :], 1.0 / DI)
            dve.memset(ones_w[:, :], 1.0).then_inc(ready0, 1)
            dve.memset(zeros[:, :], 0.0)
            dve.memset(g[:, RING - 1, :], 0.0).then_inc(ready0, 1)
            dve.wait_ge(w_loaded, 12 * DMA)
            dve.wait_ge(pe0, 1)
            dve.tensor_copy(w_proj[:, :, :, 2], b_ps[:, 0:32 * NT].rearrange("p (a b) -> p a b", b=32)).then_inc(dve0, 1)
            w_v = vec_s[:, :, 0:TAPS]
            dve.tensor_tensor(w_sum[:, :, :], w_v[:, :, 0:2], w_v[:, :, 2:4], ALU.add).then_inc(conv_step, 1)
            dve.tensor_scalar(neg_w[:, :, :], w_v, -1.0, None, ALU.mult).then_inc(conv_step, 1)
            dve.wait_ge(conv_step, 1)
            dve.tensor_tensor(w_sum[:, :, 0:1], w_sum[:, :, 0:1], w_sum[:, :, 1:2], ALU.add).then_inc(conv_step, 1)
            dve.wait_ge(conv_step, 3)
            temb = vec_s[:, :, V_TEMB:V_TEMB + B]
            dve.tensor_tensor(conv_bias[:, :, :], temb, w_sum[:, :, 0:1].to_broadcast([P, NT, B]), ALU.mult).then_inc(conv_step, 1)
            dve.wait_ge(conv_step, 4)
            dve.tensor_tensor(conv_bias[:, :, :], conv_bias[:, :, :], vec_s[:, :, V_BCONV:V_BCONV + 1].to_broadcast([P, NT, B]),
                              ALU.add)
            for quad in range(2):
                for d in range(4):
                    jh = 4 * quad + d
                    for b in range(B):
                        last = dve.tensor_scalar(taps[quad][:, d, :, b, 0:HIST],
                                                 neg_w[:, jh, :].unsqueeze(2).to_broadcast([P, TAPS, HIST]),
                                                 vec_s[:, jh, V_TEMB + b:V_TEMB + b + 1], None, ALU.mult)
            last.then_inc(dve0, 1)
            dve.wait_ge(dve0, 2)
            dve.sem_inc(taps_free, 2)

            def sum_y(k, kp, grp):
                dve.wait_ge(b_full, k * 3 + (1 if grp == 0 else 2))
                if grp == 0:
                    dve.wait_ge(dxn_ready, k + 1)
                if has(k, 1, NCH):
                    dve.wait_ge(gated, k * 2 + (grp - 1))
                dve.tensor_tensor(y_sum[grp][:, :, :], b_ps[:, :].rearrange("p (a t) -> p a t", t=GRP),
                                  d_xn[kp][:, :, :].rearrange("p a (b t) -> p (a b) t", t=T)[:, :, GRP * grp:GRP * grp + GRP],
                                  ALU.add).then_inc(y_summed, 1)
                dve.wait_ge(y_summed, k * 2 + (grp + 1))
                dve.sem_inc(b_free, 1)

            def add_x(k, kp):
                dve.wait_ge(b_full, k * 3 + 3)
                dve.wait_ge(res_loaded, (k + 1) * DMA)
                if has(k, 1, NCH):
                    dve.wait_ge(stored, k * DMA)
                dve.tensor_tensor(o_sb[kp][:, :], b_ps[:, :], x_res[:, :], ALU.add).then_inc(out_ready, 1)
                dve.wait_ge(out_ready, k + 1)
                dve.sem_inc(b_free, 1)

            def var_floor(k):
                dve.wait_ge(ln_step, k * 4 + 5)
                dve.tensor_scalar(rs[:, 0, :], rs[:, 0, :], EPS, None, ALU.max).then_inc(var_ready, 1)

            def invert_std(k):
                dve.wait_ge(std_ready, k + 2)
                dve.reciprocal(rs[:, 1, :], rs[:, 1, :]).then_inc(rstd_ready, 1)

            def run_prod(k, kp):
                dve.wait_ge(a_ready, k + 1)
                first = isinstance(k, int) and k == 0
                dve.tensor_tensor_scan(prod[:, kp, :], tmp[:, 3, :], zeros[:, :],
                                       1.0 if first else prod[:, (kp + 1) % 2, T - 1:T], ALU.mult, ALU.add).then_inc(prod_ready, 1)
                dve.wait_ge(prod_ready, k + 1)
                dve.reciprocal(inv[:, :], prod[:, kp, :]).then_inc(inv_ready, 1)
                dve.wait_ge(inv_ready, k + 1)
                dve.tensor_scalar(par[kp][:, 1, :], inv[:, :], LIM, None, ALU.mult)
                dve.tensor_scalar(par[kp][:, 2, :], inv[:, :], -LIM, None, ALU.mult)
                dve.wait_ge(bn_ready, k + 1)
                dve.scalar_tensor_tensor(out=tmp[:, 0, :], in0=tmp[:, 1, :], scalar=1.0, in1=prm[:, 0, :],
                                         op0=ALU.min, op1=ALU.mult).then_inc(u_ready, 1)
                dve.wait_ge(u_ready, k + 1)
                dve.tensor_tensor(par[kp][:, 0, :], tmp[:, 0, :], inv[:, :], ALU.mult).then_inc(par_ready, 1)

            def one(k, kp):
                np_ = (kp + 1) % 2
                if not has(k, 0, NCH - 1):
                    if k == -1:
                        var_floor(k)
                        invert_std(k)
                        run_prod(0, 0)
                    if k == NCH:
                        sum_y(k - 1, np_, 1)
                        add_x(k - 1, np_)
                    return
                first = isinstance(k, int) and k == 0
                for t in range(T):
                    if t % 2 == 0:
                        dve.wait_ge(x_bc, k * T + (t + 2))
                    if t == 0:
                        dve.wait_ge(par_ready, k + 1)
                    if not (first and t == 0):
                        dve.wait_ge(clipped, k * T + t)
                    dve.scalar_tensor_tensor(out=w[:, :], in0=xb[t % XB][:, :], scalar=par[kp][:, 0, t:t + 1],
                                             in1=g[:, (t - 1) % RING, :], op0=ALU.mult, op1=ALU.add).then_inc(x_used, 1)
                    if t % 4 == 0 and not (first and t < RING):
                        dve.wait_ge(y_batch, k * SLOTS + (t // 4 - 1))
                    dve.wait_ge(x_used, k * T + (t + 1))
                    dve.tensor_scalar(g[:, t % RING, :], w[:, :], par[kp][:, 1, t:t + 1], par[kp][:, 2, t:t + 1],
                                      ALU.min, ALU.max).then_inc(clipped, 1)
                    if t == 6 and has(k, 1, NCH):
                        sum_y(k - 1, np_, 1)
                    if t == 9 and has(k, 0, NCH - 2):
                        var_floor(k)
                    if t == 11 and has(k, 0, NCH - 2):
                        invert_std(k)
                    if t == 17 and has(k, 1, NCH):
                        add_x(k - 1, np_)
                    if t == 22:
                        sum_y(k, kp, 0)
                    if t == 27 and has(k, 0, NCH - 2):
                        run_prod(k + 1, np_)

            chunks(dve, one)

        @block.gpsimd
        def _(pool):
            for i in range(NG):
                last = pool.memset(cw[i][:, :], 0.0)
            last.then_inc(pool_step, 1)
            pool.wait_ge(pool_step, 1)
            pool.wait_ge(w_loaded, 12 * DMA)
            pool.wait_ge(dve0, 2)
            pool.wait_ge(act0, 2)

            def turn_gate(k, kp, grp):
                pool.wait_ge(y_summed, k * 2 + (grp + 1))
                pool.wait_ge(a_free, job(k, GATE1) + 1)
                if has(k, 2, NCH):
                    pool.wait_ge(b_full, k * 3 - 3)
                sl = slice(GRP * grp, GRP * grp + GRP)
                pool.tensor_tensor(yg[kp][:, :, sl], y_sum[grp][:, :, :],
                                   gate[kp][:, :, :].rearrange("p a (b t) -> p (a b) t", t=T)[:, :, sl],
                                   ALU.mult).then_inc(gated, 1)

            def c_weights(k, grp):
                if grp == 0:
                    pool.wait_ge(cp_ready, k + 1)
                if has(k, 1, NCH):
                    pool.wait_ge(y_batch, k * SLOTS - (4 if grp == 0 else 0))
                dst = cw[grp][:, :].rearrange("p (r v) -> p r v", r=4)[:, :, 0:4 * 32]
                dst = dst.rearrange("p r (c m) -> p r c m", c=4)[:, :, :, 0:8]
                src = cp[:, GRP * grp:GRP * grp + GRP].rearrange("p (r c) -> p r c", c=4).unsqueeze(3).to_broadcast([P, 4, 4, 8])
                m = mask_s[:, :].unsqueeze(1).unsqueeze(1).to_broadcast([P, 4, 4, 8])
                pool.tensor_tensor(dst, src, m, ALU.mult).then_inc(cw_ready, 1)

            def conv(c, quad):
                pool.wait_ge(a_free, job(c - 2, (XR0, XR1)[quad]) + 1)
                if has(c, 1, NCH):
                    pool.wait_ge(silu_done, c * 2 + (quad - 1))
                n = c * 8 + 4 * quad
                acc, two = cv[quad][:, :].rearrange("p (a b t) -> p a b t", a=4, b=B), cv2[:, :].rearrange("p (a b t) -> p a b t", a=4, b=B)
                tp = taps[quad]
                pool.tensor_tensor(acc, tp[:, :, 0, :, 0:T], tp[:, :, 1, :, 1:1 + T], ALU.add).then_inc(conv_step, 1)
                pool.tensor_tensor(two, tp[:, :, 2, :, 2:2 + T], tp[:, :, 3, :, 3:3 + T], ALU.add).then_inc(conv_step, 1)
                pool.wait_ge(conv_step, n + 6)
                pool.tensor_tensor(cv[quad][:, :], cv[quad][:, :], cv2[:, :], ALU.add).then_inc(conv_step, 1)
                pool.tensor_copy(tp[:, :, :, :, 0:HIST].rearrange("p a k b t -> p (a k b) t"),
                                 tp[:, :, :, :, T:T + HIST].rearrange("p a k b t -> p (a k b) t")).then_inc(taps_free, 1)
                pool.wait_ge(conv_step, n + 7)
                pool.tensor_tensor(cv[quad][:, :].rearrange("p (a t) -> p a t", t=T), cv[quad][:, :].rearrange("p (a t) -> p a t", t=T),
                                   conv_bias[:, 4 * quad:4 * quad + 4, :].rearrange("p a b -> p (a b)").unsqueeze(2).to_broadcast([P, 16, T]),
                                   ALU.add).then_inc(conv_step, 1)
                pool.wait_ge(conv_step, n + 8)
                pool.sem_inc(conv_done, 1)

            def norm(k):
                pool.wait_ge(a_free, job(k, STATS) + 1)
                n = k * 4 + 4
                pool.tensor_tensor(rs[:, 0, :], st[:, 2, :], st[:, 1, :], ALU.subtract).then_inc(ln_step, 1)
                pool.wait_ge(rstd_ready, k + 2)
                pool.tensor_tensor(rs[:, 2, :], rs[:, 1, :], st[:, 0, :], ALU.mult).then_inc(ln_step, 1)
                for quad in range(2):
                    part = xn[:, 4 * quad:4 * quad + 4, :]
                    last = pool.tensor_tensor(part, part, rs[:, 1:2, :].to_broadcast([P, 4, TOK]), ALU.mult)
                    last.then_inc(ln_step, 1)
                for quad in range(2):
                    part = xn[:, 4 * quad:4 * quad + 4, :]
                    pool.wait_ge(ln_step, n + 3 + quad)
                    pool.tensor_tensor(part, part, rs[:, 2:3, :].to_broadcast([P, 4, TOK]), ALU.subtract).then_inc(ln_done, 1)

            def splits(k):
                for h in range(2):
                    pool.wait_ge(hi_ready, k * 2 + (3 + h))
                    pool.wait_ge(tok_ready, k * 2 + (3 + h))
                    pool.tensor_tensor(x_tok[h][:, :], x_tok[h][:, :], parts[h][:, 0, :], ALU.subtract).then_inc(rem_ready, 1)
                for h in range(2):
                    pool.wait_ge(mid_ready, k * 2 + (3 + h))
                    pool.tensor_tensor(parts[h][:, 2, :], x_tok[h][:, :], parts[h][:, 1, :], ALU.subtract).then_inc(lo_ready, 1)

            def params_b(k, np_):
                pool.wait_ge(prod_ready, k + 2)
                if has(k, 0, NCH):
                    pool.wait_ge(cw_ready, k * 2 + 2)
                pool.tensor_tensor(cp[:, :], prm[:, 1, :], prod[:, np_, :], ALU.mult).then_inc(cp_ready, 1)

            def one(k, kp):
                np_ = (kp + 1) % 2
                scan, front1, front2 = has(k, 0, NCH - 1), has(k, -2, NCH - 3), has(k, -1, NCH - 2)
                if front2:
                    conv(k + 1, 1)
                if has(k, 1, NCH):
                    turn_gate(k - 1, np_, 1)
                if scan:
                    c_weights(k, 1)
                if front2:
                    norm(k)
                    splits(k)
                if scan:
                    turn_gate(k, kp, 0)
                if front2:
                    params_b(k, np_)
                    c_weights(k + 1, 0)
                if front1:
                    conv(k + 2, 0)

            chunks(pool, one)


def kernel(x, cond_2048, L0_cond_W_in, L0_cond_W_conv, L0_cond_b_conv, L0_cond_ln_g, L0_cond_ln_b, L0_cond_W_xproj,
           L0_cond_W_dt, L0_cond_b_dt, L0_cond_A_log, L0_cond_D, L0_cond_W_out):
    import ml_dtypes
    import numpy as np
    import concourse.bacc as bacc
    from concourse.bass_utils import run_bass_kernel_spmd

    def tiles(a):
        a = np.asarray(a)
        return np.ascontiguousarray(a.reshape(2, 4, P, -1).transpose(2, 1, 0, 3)).reshape(P, NT, -1)

    w_x = np.asarray(L0_cond_W_xproj)
    bc = tiles(w_x[0:2 * NS].T).reshape(P, NT, 2, NS).transpose(0, 1, 3, 2)
    bc = np.concatenate([bc, np.zeros((P, NT, NS, 1), np.float32)], axis=3)
    dtx = w_x[2 * NS:3 * NS].reshape(NS, 2, 4, P).transpose(0, 2, 1, 3).reshape(NS, NT, P)
    w_dt_t = np.asarray(L0_cond_W_dt).T
    vec = np.concatenate([tiles(L0_cond_W_conv), tiles(L0_cond_b_conv), tiles(L0_cond_ln_g), tiles(L0_cond_ln_b),
                          tiles(L0_cond_D), tiles(np.asarray(cond_2048).T)], axis=2)
    nvec = np.stack([np.tile(np.asarray(L0_cond_A_log), 8), np.tile(np.asarray(L0_cond_b_dt), 8)], axis=1)

    p = np.arange(P)
    batch, half = p // 32, p // 16 % 2
    row = np.arange(XK)
    row_batch, row_q, row_half = row // (4 * XROWS), row // XROWS % 4, row % 2
    sel = ((row_batch[:, None, None] == batch) & (row_half[:, None, None] == half)
           & (row_q[:, None, None] == np.arange(4)[:, None])).astype(ml_dtypes.bfloat16)
    mask = (np.arange(8)[None, :] == (half * 4 + batch)[:, None]).astype(np.float32)
    step_r, step_c, yh, yb = p // 8 % 4, p // 32, p // 4 % 2, p % 4
    perm = (np.arange(P)[None, :] == (yh * 64 + yb * 16 + 4 * step_r + step_c)[:, None]).astype(np.float32)

    arrays = {
        "x_d": np.asarray(x), "vec_d": vec, "w_in_d": np.asarray(L0_cond_W_in).T, "w_out_d": tiles(np.asarray(L0_cond_W_out).T),
        "w_bc_d": np.concatenate([bc, bc], axis=2), "w_dtx_d": dtx,
        "w_dt_d": np.concatenate([w_dt_t, w_dt_t], axis=1), "nvec_d": nvec, "sel_d": sel, "ident_d": np.eye(P, dtype=np.float32),
        "perm_d": perm, "mask_d": mask,
    }
    arrays = {n: np.ascontiguousarray(a) for n, a in arrays.items()}
    nc = bacc.Bacc("TRN2", target_bir_lowering=False, num_devices=1)
    aps = [nc.dram_tensor(n, a.shape, mybir.dt.from_np(a.dtype), kind="ExternalInput").ap() for n, a in arrays.items()]
    out = nc.dram_tensor("out_d", (B, S, DM), F32, kind="ExternalOutput").ap()
    build(nc, *aps, out)
    r = run_bass_kernel_spmd(nc, [arrays], core_ids=[0])
    return r.results[0]["out_d"]
```

```python
from contextlib import ExitStack

import concourse.bass as bass
from concourse import mybir

F32 = mybir.dt.float32
BF16 = mybir.dt.bfloat16
ALU = mybir.AluOpType
ACT = mybir.ActivationFunctionType

P = 128
B, S, DM, DI, NS = 4, 1024, 512, 1024, 16
TAPS = 4
T = 32
NCH = S // T
TOK = B * T
NT = DI // P
KC = DM // P
HALF = DI // 2
GRP = 16
NG = T // GRP
SLOTS = T // 4
RING = 8
XB = 4
SPLIT = 3
XROWS = 2 * SPLIT
XK = XROWS * 4 * B
PRM_DMAS = 2 * B
EPS = 1e-5
LIM = 10.0
HIST = TAPS - 1
DMA = 16
XW = 3
V_AT, Y1_AT, X_AT, Y0_AT = (3, 4, 6), 5, 25, 30
PR_AT = (24, 26, 27, 28, 29, 31)

STATS, XT, XR0, PROJ, TOK0, TOK1, XR1, GATE0, GATE1 = range(9)
V_BCONV, V_G, V_B, V_D, V_TEMB, V_ALL = TAPS, TAPS + 1, TAPS + 2, TAPS + 3, TAPS + 4, TAPS + 4 + B


def job(k, place):
    if isinstance(k, int):
        if k == -2:
            return (XT, XR0, XR1).index(place)
        if k == NCH - 2:
            return 9 * k + 12 + (STATS, PROJ, TOK0, TOK1, GATE0, GATE1).index(place)
    return k * 9 + (12 + place)


def job_bank(k, par, place):
    return job(k, place) % 2 if isinstance(k, int) else (par + place) % 2


def build(nc, x, vec, w_in, w_out, w_bc, w_dtx, w_dt, nvec, sel, ident, perm, mask, out):
    with ExitStack() as ctx:
        def sb(name, shape, dt=F32):
            return ctx.enter_context(nc.sbuf_tensor(name, shape, dt))

        def ps(name):
            return ctx.enter_context(nc.psum_tensor(name, [P, 512], F32))

        def sem(name):
            return ctx.enter_context(nc.semaphore(name))

        w_in_s = sb("w_in_s", [P, KC, 2 * DI])
        w_out_s = sb("w_out_s", [P, NT, DM])
        w_proj = sb("w_proj", [P, NT, 32, 3])
        w_dtx_s = sb("w_dtx_s", [NS, NT, P])
        w_dt_s = sb("w_dt_s", [NS, 32])
        vec_s = sb("vec_s", [P, NT, V_ALL])
        nvec_s = sb("nvec_s", [P, 2])
        neg_a = sb("neg_a", [P, 2])
        sel_s = sb("sel_s", [XK, 4, P], BF16)
        ident_s = sb("ident_s", [P, P])
        perm_s = sb("perm_s", [P, P])
        mask_s = sb("mask_s", [P, 8])
        mean_w = sb("mean_w", [P, 32])
        pick_w = sb("pick_w", [P, P])
        ones_w = sb("ones_w", [P, 32])
        zeros = sb("zeros", [P, T])
        conv_bias = sb("conv_bias", [P, NT, B])
        neg_w = sb("neg_w", [P, NT, TAPS])
        w_sum = sb("w_sum", [P, NT, 2])
        x_in = sb("x_in", [P, DM])
        x_t = sb("x_t", [P, 2, KC, TOK])
        taps = [sb(f"taps{q}", [P, 4, TAPS, B, HIST + T]) for q in range(2)]
        cv = [sb(f"cv{q}", [P, 512]) for q in range(2)]
        cv2 = sb("cv2", [P, 512])
        xn = sb("xn", [P, NT, TOK])
        sq = sb("sq", [P, NT, TOK])
        st = sb("st", [P, 3, TOK])
        st_part = sb("st_part", [P, 2 * TOK])
        rs = sb("rs", [P, 2, TOK])
        d_xn = [sb(f"d_xn{i}", [P, NT, TOK]) for i in range(2)]
        gate = [sb(f"gate{i}", [P, NT, TOK]) for i in range(2)]
        pr = sb("pr", [P, TOK])
        x_tok = [sb(f"x_tok{h}", [P, 512]) for h in range(2)]
        rem = sb("rem", [P, 512])
        parts = [sb(f"parts{h}", [P, SPLIT, 512], BF16) for h in range(2)]
        xs = [sb(f"xs{i}", [XK, T // 4, 512], BF16) for i in range(2)]
        prm = sb("prm", [P, 4, T])
        tmp = sb("tmp", [P, 4, T])
        prod = sb("prod", [P, 2, T])
        inv = sb("inv", [P, T])
        cp = sb("cp", [P, T])
        par = [sb(f"par{i}", [P, 3, T]) for i in range(2)]
        cw = [sb(f"cw{g}", [P, 4 * (4 * 32 + 8)]) for g in range(NG)]
        w = sb("w", [P, 512])
        g = sb("g", [P, RING, 512])
        y_row = [sb(f"y_row{i}", [P, 512]) for i in range(2)]
        y_sum = [sb(f"y_sum{i}", [P, 32, GRP]) for i in range(2)]
        yg = [sb(f"yg{i}", [P, NT * B, T]) for i in range(2)]
        x_res = sb("x_res", [P, DM])
        o_sb = [sb(f"o_sb{i}", [P, DM]) for i in range(2)]

        xb = [ps(f"xb{i}") for i in range(XB)]
        y_ps = ps("y_ps")
        a_ps = [ps(f"a_ps{i}") for i in range(2)]
        b_ps = ps("b_ps")

        w_loaded, ready0 = sem("w_loaded"), sem("ready0")
        x_loaded, res_loaded, prm_loaded, xs_loaded, stored = (
            sem(n) for n in ("x_loaded", "res_loaded", "prm_loaded", "xs_loaded", "stored"))
        a_full, a_free, b_full = (sem(n) for n in ("a_full", "a_free", "b_full"))
        xt_ready, taps_ready, taps_free, conv_done, silu_done, sq_done = (
            sem(n) for n in ("xt_ready", "taps_ready", "taps_free", "conv_done", "silu_done", "sq_done"))
        var_step, ln_step, ln_done, xn_ready, sq_n_done, dxn_ready, gate_ready = (
            sem(n) for n in ("var_step", "ln_step", "ln_done", "xn_ready", "sq_n_done", "dxn_ready", "gate_ready"))
        pr_ready, tok_ready, hi_ready, rem_ready, mid_ready, lo_ready = (
            sem(n) for n in ("pr_ready", "tok_ready", "hi_ready", "rem_ready", "mid_ready", "lo_ready"))
        th_ready, a_ready, prod_ready, inv_ready, par_ready, cp_ready, cw_ready, pool_step = (
            sem(n) for n in ("th_ready", "a_ready", "prod_ready", "inv_ready", "par_ready", "cp_ready", "cw_ready", "pool_step"))
        x_bc, x_used, clipped, y_batch, y_rows, y_summed, gated, out_ready = (
            sem(n) for n in ("x_bc", "x_used", "clipped", "y_batch", "y_rows", "y_summed", "gated", "out_ready"))
        conv_step, dve0, act0, pe0 = sem("conv_step"), sem("dve0"), sem("act0"), sem("pe0")
        partial_full, partial_ready = sem("partial_full"), sem("partial_ready")
        bn_ready, u_ready, var_ready, std_ready, rstd_ready = (sem(n) for n in ("bn_ready", "u_ready", "var_ready", "std_ready", "rstd_ready"))

        def chan(jh):
            return (jh % 2) * HALF + (jh // 2) * P

        def chunks(eng, one):
            first = 3
            for k in range(-2, first):
                one(k, k % 2)
            turns = (NCH - 3 - first) // 2
            with eng.Fori(0, turns) as i:
                one(i * 2 + first, first % 2)
                one(i * 2 + (first + 1), (first + 1) % 2)
            for k in range(first + 2 * turns, NCH + 1):
                one(k, k % 2)

        def has(k, lo, hi):
            return lo <= k <= hi if isinstance(k, int) else True

        block = ctx.enter_context(nc.Block())

        @block.sync
        def _(sp):
            for dst, src in ((x_in[:, :], x[:, 0:T, :]), (w_in_s[:, :, 0:DI], w_in.rearrange("(c p) n -> p c n", p=P)[:, :, 0:DI]),
                             (vec_s[:, :, :], vec), (ident_s[:, :], ident), (w_proj[:, :, :, :], w_bc),
                             (w_dtx_s[:, :, :], w_dtx), (w_dt_s[:, :], w_dt), (nvec_s[:, :], nvec),
                             (sel_s[:, :, :], sel), (perm_s[:, :], perm), (mask_s[:, :], mask),
                             (w_in_s[:, :, DI:2 * DI], w_in.rearrange("(c p) n -> p c n", p=P)[:, :, DI:2 * DI]),
                             (w_out_s[:, :, :], w_out)):
                d = sp.dma_start(dst, src)
                d.then_inc(x_loaded if dst.tensor.name == x_in.name else w_loaded, DMA)

            def one(k, kp):
                np_ = (kp + 1) % 2

                def val(v):
                    return v if isinstance(v, int) else sp.snap(v)

                k0, k1, k2, steps = val(k), val(k + 1), val(k + 2), val(k * T)
                lo_h = [val(k * 2 + (3 + h)) for h in range(2)]
                turned = val(job(k, XT) + 1) if has(k, -2, NCH - 3) else None
                at_prev, at_this, at_next = val((k - 1) * T), val(k * T), val((k + 3) * T)
                if has(k, -2, NCH - 4):
                    sp.wait_ge(a_full, turned)
                    sp.dma_start(x_in[:, :], x[:, bass.ds(at_next, T), :]).then_inc(x_loaded, DMA)
                if has(k, -1, NCH - 2):
                    sp.wait_ge(pr_ready, k2)
                    for b in range(B):
                        sp.dma_start(prm[32 * b:32 * b + 32, 0:3, :], pr[0:96, T * b:T * b + T]).then_inc(prm_loaded, DMA)
                        sp.dma_start(prm[32 * b:32 * b + 32, 3, :], pr[96:P, T * b:T * b + T]).then_inc(prm_loaded, DMA)
                    if has(k, 1, NCH):
                        sp.wait_ge(x_bc, steps)
                    for h in range(2):
                        sp.wait_ge(lo_ready, lo_h[h])
                        wide = xs[np_][:, :, :].ap[0][0]
                        for part in range(SPLIT):
                            rows = bass.AP(tensor=xs[np_][:, :, :].tensor, offset=(2 * part + h) * wide,
                                           ap=[[XROWS * wide, 4 * B], [512, T // 4], [1, 512]])
                            sp.dma_start(rows, parts[h][:, part, :]).then_inc(xs_loaded, DMA)
                if has(k, 1, NCH):
                    sp.wait_ge(out_ready, k0)
                    sp.dma_start(out[:, bass.ds(at_prev, T), :], o_sb[np_][:, :]).then_inc(stored, DMA)
                if has(k, 0, NCH - 1):
                    sp.dma_start(x_res[:, :], x[:, bass.ds(at_this, T), :]).then_inc(res_loaded, DMA)

            chunks(sp, one)
            sp.wait_ge(stored, DMA * NCH)

        @block.tensor
        def _(pe):
            def open_job(k, place):
                n = job(k, place)
                if not isinstance(n, int) or n >= 2:
                    pe.wait_ge(a_free, n - 1)

            def in_quad(k, kp, chunk_par, place, quad, col0, s):
                if s == 0:
                    open_job(k, place)
                jh = 4 * quad + s
                for c in range(KC):
                    mm = pe.matmul(a_ps[job_bank(k, kp, place)][:, TOK * s:TOK * s + TOK],
                                   w_in_s[:, c, col0 + chan(jh):col0 + chan(jh) + P],
                                   x_t[:, chunk_par, c, :], start=(c == 0), stop=(c == KC - 1))
                if s == 3:
                    mm.then_inc(a_full, 1)

            def x_transpose(k, kp):
                open_job(k, XT)
                pe.wait_ge(x_loaded, (k + 3) * DMA)
                for c in range(KC):
                    mm = pe.transpose(a_ps[job_bank(k, kp, XT)][:, TOK * c:TOK * c + TOK],
                                      x_in[:, P * c:P * c + P], ident_s[:, :])
                mm.then_inc(a_full, 1)

            def bring_x(k, kp, t):
                q = t // (T // 4)
                if isinstance(k, int) and k == 0 and t < XB:
                    pass
                else:
                    pe.wait_ge(x_used, k * T + (t - XB + 1))
                pe.matmul(xb[t % XB][:, :], sel_s[:, q, :], xs[kp][:, t % (T // 4), :],
                          start=True, stop=True).then_inc(x_bc, 1)

            def contract(k, slot):
                grp, r = slot // 4, slot % 4
                pe.wait_ge(clipped, k * T + 4 * slot + 4)
                if r == 0:
                    if grp == 0:
                        pe.wait_ge(cw_ready, k * 2 + 1)
                    else:
                        pe.wait_ge(cw_ready, k * 2 + 2)
                    if not (isinstance(k, int) and k == 0 and grp == 0):
                        pe.wait_ge(y_rows, k * 2 + grp)
                for c in range(4):
                    t = 4 * slot + c
                    s = 4 * r + c
                    mm = pe.matmul(y_ps[32 * c:32 * c + 32, :], cw[grp][:, 32 * s:32 * s + 32], g[:, t % RING, :],
                                   start=(r == 0), stop=(r == 3), tile_position=(0, 32 * c))
                mm.then_inc(y_batch, 1)

            def y_turn(k, grp):
                pe.wait_ge(y_rows, k * 2 + (grp + 1))
                if grp == 1:
                    pe.wait_ge(y_summed, k * 2 + 1)
                elif not (isinstance(k, int) and k == 0):
                    pe.wait_ge(out_ready, k)
                for j in range(4):
                    mm = pe.transpose(b_ps[:, P * j:P * j + P], y_row[grp][:, P * j:P * j + P], perm_s[:, :])
                mm.then_inc(b_full, 1)

            def out_part(k, kp, quarter):
                if quarter == 0:
                    pe.wait_ge(gated, k * 2 + 2)
                    if isinstance(k, int) and k == 0:
                        pe.wait_ge(w_loaded, 12 * DMA)
                jh = quarter
                mm = pe.matmul(b_ps[:, :], yg[kp][:, B * jh:B * jh + B, :], w_out_s[:, jh, :],
                               start=(jh == 0), stop=(jh == NT - 1))
                if jh == NT - 1:
                    mm.then_inc(b_full, 1)

            def stats_partial(k, kp):
                open_job(k, STATS)
                pe.wait_ge(sq_done, k * 2 + 4)
                for part, src in ((0, xn), (1, sq)):
                    for jh in range(NT):
                        c = jh % 4
                        mm = pe.matmul(a_ps[job_bank(k, kp, STATS)][32 * c:32 * c + 32, TOK * part:TOK * part + TOK],
                                       mean_w[:, :], src[:, jh, :], start=(jh < 4), stop=(jh >= 4), tile_position=(0, 32 * c))
                mm.then_inc(partial_full, 1)

            def stats_total(k, kp):
                pe.wait_ge(partial_ready, k + 2)
                pe.matmul(a_ps[job_bank(k, kp, STATS)][:, 2 * TOK:4 * TOK], pick_w[:, :], st_part[:, :],
                          start=True, stop=True).then_inc(a_full, 1)

            def project(k, kp, part):
                if part == 0:
                    open_job(k, PROJ)
                    pe.wait_ge(sq_n_done, k * 2 + 4)
                for jh in range(4 * part, 4 * part + 4):
                    for kind in range(4):
                        lhs = w_cols[:, jh, 32 * kind:32 * kind + 32] if kind < 3 else ones_w[:, :]
                        mm = pe.matmul(a_ps[job_bank(k, kp, PROJ)][32 * kind:32 * kind + 32, 0:TOK], lhs,
                                       (xn if kind < 3 else sq)[:, jh, :], start=(jh == 0), stop=(jh == NT - 1),
                                       tile_position=(0, 32 * kind))
                if part == 1:
                    mm.then_inc(a_full, 1)

            w_cols = w_proj[:, :, :, :].rearrange("p a s k -> p a (s k)")

            def to_tokens(k, kp, h):
                place = (TOK0, TOK1)[h]
                open_job(k, place)
                for j in range(4):
                    mm = pe.transpose(a_ps[job_bank(k, kp, place)][:, P * j:P * j + P], xn[:, 2 * j + h, :], ident_s[:, :])
                mm.then_inc(a_full, 1)

            pe.wait_ge(w_loaded, 12 * DMA)
            pe.wait_ge(ready0, 2)
            for jh in range(NT):
                mm = pe.matmul(b_ps[:, 32 * jh:32 * jh + 32], w_dtx_s[:, jh, :], w_dt_s[:, :], start=True, stop=True)
            mm.then_inc(pe0, 1)
            pe.wait_ge(dve0, 1)

            def one(k, kp):
                np_ = (kp + 1) % 2
                scan, front1, front2 = has(k, 0, NCH - 1), has(k, -2, NCH - 3), has(k, -1, NCH - 2)
                back = has(k, 1, NCH)
                for slot in range(SLOTS):
                    for s in range(4):
                        t = 4 * slot + s
                        if scan:
                            if t == 0 and isinstance(k, int) and k == 0:
                                pe.wait_ge(xs_loaded, 2 * SPLIT * DMA)
                                for first in range(XB - 1):
                                    bring_x(k, kp, first)
                            if t + XB - 1 < T:
                                bring_x(k, kp, t + XB - 1)
                            elif has(k, 0, NCH - 2):
                                if t + XB - 1 == T:
                                    pe.wait_ge(xs_loaded, (k + 2) * (2 * SPLIT * DMA))
                                bring_x(k + 1, np_, t + XB - 1 - T)
                        if s == 1:
                            if slot == 0 and back:
                                contract(k - 1, SLOTS - 1)
                            if slot > 0 and scan:
                                contract(k, slot - 1)
                        if slot == 0 and s == 0 and front2:
                            stats_partial(k, kp)
                        if slot == 0 and s == 2 and front2:
                            stats_total(k, kp)
                        if slot == 0 and s == 3 and front1:
                            x_transpose(k, kp)
                        if slot == 1 and s == 0 and back:
                            y_turn(k - 1, 1)
                        if slot == 1 and front1:
                            if s == 0:
                                pe.wait_ge(xt_ready, k + 3)
                            in_quad(k, kp, kp, XR0, 0, 0, s)
                        if slot in (2, 5) and back:
                            out_part(k - 1, np_, 4 * (slot == 5) + s)
                        if slot == 3 and s < 2 and front2:
                            project(k, kp, s)
                        if slot == 3 and s >= 2 and front2:
                            to_tokens(k, kp, s - 2)
                        if slot == 4 and front1:
                            in_quad(k, kp, kp, XR1, 1, 0, s)
                        if slot == 6 and front2:
                            in_quad(k, kp, np_, GATE0, 0, DI, s)
                        if slot == 6 and s == 3 and scan:
                            y_turn(k, 0)
                        if slot == 7 and front2:
                            in_quad(k, kp, np_, GATE1, 1, DI, s)

            chunks(pe, one)

        @block.scalar
        def _(act):
            def take(k, kp, place):
                act.wait_ge(a_full, job(k, place) + 1)
                return a_ps[job_bank(k, kp, place)]

            act.wait_ge(w_loaded, 12 * DMA)
            act.activation(neg_a[:, 0:1], nvec_s[:, 0:1], ACT.Tanh).then_inc(act0, 1)
            act.wait_ge(act0, 1)
            act.activation(neg_a[:, 1:2], neg_a[:, 0:1], ACT.Copy, scale=-0.01).then_inc(act0, 1)
            act.wait_ge(act0, 2)
            act.wait_ge(dve0, 2)

            def gates(k, kp, place, quad, chunk_par):
                src = take(k, kp, place)
                if has(k, 1, NCH):
                    act.wait_ge(gated, k * 2)
                act.activation(gate[chunk_par][:, 4 * quad:4 * quad + 4, :].rearrange("p a b -> p (a b)"), src[:, :],
                               ACT.Silu).then_inc(a_free, 1)

            def rows_out(k, grp):
                act.wait_ge(y_batch, k * SLOTS + 4 * (grp + 1))
                if has(k, 1, NCH):
                    act.wait_ge(b_full, k * 3 - (2 if grp == 0 else 1))
                act.activation(y_row[grp][:, :], y_ps[:, :], ACT.Copy).then_inc(y_rows, 1)

            def silu(c, quad):
                act.wait_ge(conv_done, c * 2 + (quad + 1))
                part = xn[:, 4 * quad:4 * quad + 4, :].rearrange("p a b -> p (a b)")
                act.activation(part, cv[quad][:, :], ACT.Silu).then_inc(silu_done, 1)
                act.wait_ge(silu_done, c * 2 + (quad + 1))
                act.activation(sq[:, 4 * quad:4 * quad + 4, :].rearrange("p a b -> p (a b)"), part,
                               ACT.Square).then_inc(sq_done, 1)

            def tap_products(k, kp, quad):
                src = take(k, kp, (XR0, XR1)[quad])
                act.wait_ge(taps_free, k * 2 + (4 + quad + 1))
                for d in range(4):
                    for tap in range(TAPS):
                        last = act.activation(taps[quad][:, d, tap, :, HIST:HIST + T],
                                              src[:, TOK * d:TOK * d + TOK].rearrange("p (b t) -> p b t", b=B),
                                              ACT.Copy, scale=vec_s[:, 4 * quad + d, tap:tap + 1])
                last.then_inc(a_free, 1)

            def one(k, kp):
                np_ = (kp + 1) % 2
                scan, front1, front2 = has(k, 0, NCH - 1), has(k, -2, NCH - 3), has(k, -1, NCH - 2)
                back = has(k, 1, NCH)
                if front2:
                    act.wait_ge(partial_full, k + 2)
                    bank = a_ps[job_bank(k, kp, STATS)]
                    act.activation(st_part[:, :], bank[:, 0:2 * TOK], ACT.Copy).then_inc(partial_ready, 1)
                if back:
                    rows_out(k - 1, 1)
                if front2:
                    src = take(k, kp, STATS)
                    act.activation(st[:, 0, :], src[:, 2 * TOK:3 * TOK], ACT.Copy)
                    act.activation(st[:, 1, :], src[:, 2 * TOK:3 * TOK], ACT.Square)
                    act.activation(st[:, 2, :], src[:, 3 * TOK:4 * TOK], ACT.Copy, bias=EPS).then_inc(a_free, 1)
                if front1:
                    src = take(k, kp, XT)
                    act.activation(x_t[:, kp, :, :].rearrange("p a b -> p (a b)"), src[:, :], ACT.Copy).then_inc(xt_ready, 1)
                    act.wait_ge(xt_ready, k + 3)
                    act.sem_inc(a_free, 1)
                if front2:
                    act.wait_ge(var_ready, k + 2)
                    act.activation(rs[:, 1, :], rs[:, 0, :], ACT.Sqrt).then_inc(std_ready, 1)
                    for quad in range(2):
                        act.wait_ge(ln_done, k * 2 + (3 + quad))
                        for jh in range(4 * quad, 4 * quad + 4):
                            last = act.activation(xn[:, jh, :], xn[:, jh, :], ACT.Identity, bias=vec_s[:, jh, V_B:V_B + 1],
                                                  scale=vec_s[:, jh, V_G:V_G + 1])
                        last.then_inc(xn_ready, 1)
                        act.wait_ge(xn_ready, k * 2 + (3 + quad))
                        act.activation(sq[:, 4 * quad:4 * quad + 4, :].rearrange("p a b -> p (a b)"),
                                       xn[:, 4 * quad:4 * quad + 4, :].rearrange("p a b -> p (a b)"),
                                       ACT.Square).then_inc(sq_n_done, 1)
                if front1:
                    tap_products(k, kp, 0)
                if front2:
                    src = take(k, kp, PROJ)
                    if has(k, 0, NCH):
                        act.wait_ge(prm_loaded, (k + 1) * (PRM_DMAS * DMA))
                    act.activation(pr[:, :], src[:, 0:TOK], ACT.Copy).then_inc(pr_ready, 1)
                    act.wait_ge(pr_ready, k + 2)
                    act.sem_inc(a_free, 1)
                    for h in range(2):
                        src = take(k, kp, (TOK0, TOK1)[h])
                        if has(k, 0, NCH):
                            act.wait_ge(lo_ready, k * 2 + (h + 1))
                            act.wait_ge(xs_loaded, (k + 1) * (2 * SPLIT * DMA))
                        act.activation(x_tok[h][:, :], src[:, :], ACT.Copy).then_inc(tok_ready, 1)
                        act.activation(parts[h][:, 0, :], src[:, :], ACT.Copy).then_inc(hi_ready, 1)
                        act.wait_ge(hi_ready, k * 2 + (3 + h))
                        act.wait_ge(tok_ready, k * 2 + (3 + h))
                        act.sem_inc(a_free, 1)
                    if has(k, 1, NCH):
                        act.wait_ge(y_summed, k * 2)
                    for jh in range(NT):
                        last = act.activation(d_xn[np_][:, jh, :], xn[:, jh, :], ACT.Copy, scale=vec_s[:, jh, V_D:V_D + 1])
                    last.then_inc(dxn_ready, 1)
                if scan:
                    rows_out(k, 0)
                if front2:
                    for h in range(2):
                        act.wait_ge(rem_ready, k * 2 + (3 + h))
                        act.activation(parts[h][:, 1, :], x_tok[h][:, :], ACT.Copy).then_inc(mid_ready, 1)
                    act.wait_ge(prm_loaded, (k + 2) * (PRM_DMAS * DMA))
                    act.activation(tmp[:, 2, :], prm[:, 2, :], ACT.Tanh, bias=nvec_s[:, 1:2]).then_inc(th_ready, 1)
                    act.wait_ge(th_ready, k + 2)
                    act.activation(tmp[:, 3, :], tmp[:, 2, :], ACT.Copy, scale=neg_a[:, 1:2], bias=1.0).then_inc(a_ready, 1)
                    act.activation(tmp[:, 1, :], prm[:, 3, :], ACT.Sqrt).then_inc(bn_ready, 1)
                if front1:
                    tap_products(k, kp, 1)
                    for quad in range(2):
                        silu(k + 2, quad)
                if front2:
                    gates(k, kp, GATE0, 0, np_)
                    gates(k, kp, GATE1, 1, np_)

            chunks(act, one)

        @block.vector
        def _(dve):
            dve.memset(mean_w[:, :], 1.0 / DI)
            dve.memset(pick_w[:, :], 0.0).then_inc(var_step, 1)
            dve.wait_ge(var_step, 1)
            for c in range(4):
                last = dve.memset(pick_w[32 * c:32 * c + 1, :], 1.0)
            dve.memset(ones_w[:, :], 1.0).then_inc(ready0, 1)
            dve.memset(zeros[:, :], 0.0)
            dve.memset(g[:, RING - 1, :], 0.0).then_inc(ready0, 1)
            dve.wait_ge(w_loaded, 12 * DMA)
            dve.wait_ge(pe0, 1)
            dve.tensor_copy(w_proj[:, :, :, 2], b_ps[:, 0:32 * NT].rearrange("p (a b) -> p a b", b=32)).then_inc(dve0, 1)
            w_v = vec_s[:, :, 0:TAPS]
            dve.tensor_tensor(w_sum[:, :, :], w_v[:, :, 0:2], w_v[:, :, 2:4], ALU.add).then_inc(conv_step, 1)
            dve.tensor_scalar(neg_w[:, :, :], w_v, -1.0, None, ALU.mult).then_inc(conv_step, 1)
            dve.wait_ge(conv_step, 1)
            dve.tensor_tensor(w_sum[:, :, 0:1], w_sum[:, :, 0:1], w_sum[:, :, 1:2], ALU.add).then_inc(conv_step, 1)
            dve.wait_ge(conv_step, 3)
            temb = vec_s[:, :, V_TEMB:V_TEMB + B]
            dve.tensor_tensor(conv_bias[:, :, :], temb, w_sum[:, :, 0:1].to_broadcast([P, NT, B]), ALU.mult).then_inc(conv_step, 1)
            dve.wait_ge(conv_step, 4)
            dve.tensor_tensor(conv_bias[:, :, :], conv_bias[:, :, :], vec_s[:, :, V_BCONV:V_BCONV + 1].to_broadcast([P, NT, B]),
                              ALU.add)
            for quad in range(2):
                for d in range(4):
                    jh = 4 * quad + d
                    for b in range(B):
                        last = dve.tensor_scalar(taps[quad][:, d, :, b, 0:HIST],
                                                 neg_w[:, jh, :].unsqueeze(2).to_broadcast([P, TAPS, HIST]),
                                                 vec_s[:, jh, V_TEMB + b:V_TEMB + b + 1], None, ALU.mult)
            last.then_inc(dve0, 1)
            dve.wait_ge(dve0, 2)
            dve.sem_inc(taps_free, 2)

            def sum_y(k, kp, grp):
                dve.wait_ge(b_full, k * 3 + (1 if grp == 0 else 2))
                if grp == 0:
                    dve.wait_ge(dxn_ready, k + 1)
                if has(k, 1, NCH):
                    dve.wait_ge(gated, k * 2 + (grp - 1))
                dve.tensor_tensor(y_sum[grp][:, :, :], b_ps[:, :].rearrange("p (a t) -> p a t", t=GRP),
                                  d_xn[kp][:, :, :].rearrange("p a (b t) -> p (a b) t", t=T)[:, :, GRP * grp:GRP * grp + GRP],
                                  ALU.add).then_inc(y_summed, 1)

            def add_x(k, kp):
                dve.wait_ge(b_full, k * 3 + 3)
                dve.wait_ge(res_loaded, (k + 1) * DMA)
                if has(k, 1, NCH):
                    dve.wait_ge(stored, k * DMA)
                dve.tensor_tensor(o_sb[kp][:, :], b_ps[:, :], x_res[:, :], ALU.add).then_inc(out_ready, 1)

            def variance(k, piece):
                if piece == 0:
                    dve.wait_ge(a_free, job(k, STATS) + 1)
                    dve.tensor_tensor(rs[:, 0, :], st[:, 2, :], st[:, 1, :], ALU.subtract).then_inc(var_step, 1)
                elif piece == 1:
                    dve.wait_ge(var_step, k + 3)
                    dve.tensor_scalar(rs[:, 0, :], rs[:, 0, :], EPS, None, ALU.max).then_inc(var_ready, 1)
                else:
                    dve.wait_ge(std_ready, k + 2)
                    dve.reciprocal(rs[:, 1, :], rs[:, 1, :]).then_inc(rstd_ready, 1)

            def run_prod(k, kp, piece):
                if piece == 0:
                    dve.wait_ge(a_ready, k + 1)
                    first = isinstance(k, int) and k == 0
                    dve.tensor_tensor_scan(prod[:, kp, :], tmp[:, 3, :], zeros[:, :],
                                           1.0 if first else prod[:, (kp + 1) % 2, T - 1:T], ALU.mult, ALU.add).then_inc(prod_ready, 1)
                elif piece == 1:
                    dve.wait_ge(prod_ready, k + 1)
                    dve.reciprocal(inv[:, :], prod[:, kp, :]).then_inc(inv_ready, 1)
                elif piece == 2:
                    dve.wait_ge(bn_ready, k + 1)
                    dve.scalar_tensor_tensor(out=tmp[:, 0, :], in0=tmp[:, 1, :], scalar=1.0, in1=prm[:, 0, :],
                                             op0=ALU.min, op1=ALU.mult).then_inc(u_ready, 1)
                elif piece == 3:
                    dve.wait_ge(inv_ready, k + 1)
                    dve.tensor_scalar(par[kp][:, 1, :], inv[:, :], LIM, None, ALU.mult)
                elif piece == 4:
                    dve.tensor_scalar(par[kp][:, 2, :], inv[:, :], -LIM, None, ALU.mult)
                else:
                    dve.wait_ge(u_ready, k + 1)
                    dve.tensor_tensor(par[kp][:, 0, :], tmp[:, 0, :], inv[:, :], ALU.mult).then_inc(par_ready, 1)

            def one(k, kp):
                np_ = (kp + 1) % 2
                if not has(k, 0, NCH - 1):
                    if k == -1:
                        for piece in range(3):
                            variance(k, piece)
                        for piece in range(6):
                            run_prod(0, 0, piece)
                    if k == NCH:
                        sum_y(k - 1, np_, 1)
                        add_x(k - 1, np_)
                    return
                first = isinstance(k, int) and k == 0
                for t in range(T):
                    if t % XW == 0:
                        dve.wait_ge(x_bc, k * T + min(t + XW, T))
                    if t == 0:
                        dve.wait_ge(par_ready, k + 1)
                    if not (first and t == 0):
                        dve.wait_ge(clipped, k * T + t)
                    dve.scalar_tensor_tensor(out=w[:, :], in0=xb[t % XB][:, :], scalar=par[kp][:, 0, t:t + 1],
                                             in1=g[:, (t - 1) % RING, :], op0=ALU.mult, op1=ALU.add).then_inc(x_used, 1)
                    if has(k, 0, NCH - 2):
                        if t in V_AT:
                            variance(k, V_AT.index(t))
                        if t in PR_AT:
                            run_prod(k + 1, np_, PR_AT.index(t))
                    if has(k, 1, NCH):
                        if t == Y1_AT:
                            sum_y(k - 1, np_, 1)
                        if t == X_AT:
                            add_x(k - 1, np_)
                    if t == Y0_AT:
                        sum_y(k, kp, 0)
                    if t % 4 == 0 and not (first and t < RING):
                        dve.wait_ge(y_batch, k * SLOTS + (t // 4 - 1))
                    dve.wait_ge(x_used, k * T + (t + 1))
                    dve.tensor_scalar(g[:, t % RING, :], w[:, :], par[kp][:, 1, t:t + 1], par[kp][:, 2, t:t + 1],
                                      ALU.min, ALU.max).then_inc(clipped, 1)

            chunks(dve, one)

        @block.gpsimd
        def _(pool):
            for i in range(NG):
                last = pool.memset(cw[i][:, :], 0.0)
            last.then_inc(pool_step, 1)
            pool.wait_ge(pool_step, 1)
            pool.wait_ge(w_loaded, 12 * DMA)
            pool.wait_ge(dve0, 2)
            pool.wait_ge(act0, 2)

            def turn_gate(k, kp, grp):
                pool.wait_ge(y_summed, k * 2 + (grp + 1))
                pool.wait_ge(a_free, job(k - 1, GATE1) + 1)
                if has(k, 2, NCH):
                    pool.wait_ge(b_full, k * 3 - 3)
                sl = slice(GRP * grp, GRP * grp + GRP)
                pool.tensor_tensor(yg[kp][:, :, sl], y_sum[grp][:, :, :],
                                   gate[kp][:, :, :].rearrange("p a (b t) -> p (a b) t", t=T)[:, :, sl],
                                   ALU.mult).then_inc(gated, 1)

            def c_weights(k, grp):
                if grp == 0:
                    pool.wait_ge(cp_ready, k + 1)
                if has(k, 1, NCH):
                    pool.wait_ge(y_batch, k * SLOTS - (4 if grp == 0 else 0))
                dst = cw[grp][:, :].rearrange("p (r v) -> p r v", r=4)[:, :, 0:4 * 32]
                dst = dst.rearrange("p r (c m) -> p r c m", c=4)[:, :, :, 0:8]
                src = cp[:, GRP * grp:GRP * grp + GRP].rearrange("p (r c) -> p r c", c=4).unsqueeze(3).to_broadcast([P, 4, 4, 8])
                m = mask_s[:, :].unsqueeze(1).unsqueeze(1).to_broadcast([P, 4, 4, 8])
                pool.tensor_tensor(dst, src, m, ALU.mult).then_inc(cw_ready, 1)

            def conv(c, quad):
                pool.wait_ge(a_free, job(c - 2, (XR0, XR1)[quad]) + 1)
                if has(c, 1, NCH):
                    pool.wait_ge(silu_done, c * 2 + (quad - 1))
                n = c * 8 + 4 * quad
                acc, two = cv[quad][:, :].rearrange("p (a b t) -> p a b t", a=4, b=B), cv2[:, :].rearrange("p (a b t) -> p a b t", a=4, b=B)
                tp = taps[quad]
                pool.tensor_tensor(acc, tp[:, :, 0, :, 0:T], tp[:, :, 1, :, 1:1 + T], ALU.add).then_inc(conv_step, 1)
                pool.tensor_tensor(two, tp[:, :, 2, :, 2:2 + T], tp[:, :, 3, :, 3:3 + T], ALU.add).then_inc(conv_step, 1)
                pool.wait_ge(conv_step, n + 6)
                pool.tensor_tensor(cv[quad][:, :], cv[quad][:, :], cv2[:, :], ALU.add).then_inc(conv_step, 1)
                pool.tensor_copy(tp[:, :, :, :, 0:HIST].rearrange("p a k b t -> p (a k b) t"),
                                 tp[:, :, :, :, T:T + HIST].rearrange("p a k b t -> p (a k b) t")).then_inc(taps_free, 1)
                pool.wait_ge(conv_step, n + 7)
                pool.tensor_tensor(cv[quad][:, :].rearrange("p (a t) -> p a t", t=T), cv[quad][:, :].rearrange("p (a t) -> p a t", t=T),
                                   conv_bias[:, 4 * quad:4 * quad + 4, :].rearrange("p a b -> p (a b)").unsqueeze(2).to_broadcast([P, 16, T]),
                                   ALU.add).then_inc(conv_step, 1)
                pool.wait_ge(conv_step, n + 8)
                pool.sem_inc(conv_done, 1)

            def center(k):
                pool.wait_ge(a_free, job(k, STATS) + 1)
                for quad in range(2):
                    part = xn[:, 4 * quad:4 * quad + 4, :]
                    pool.tensor_tensor(part, part, st[:, 0:1, :].to_broadcast([P, 4, TOK]), ALU.subtract).then_inc(ln_step, 1)

            def scale(k):
                pool.wait_ge(rstd_ready, k + 2)
                for quad in range(2):
                    part = xn[:, 4 * quad:4 * quad + 4, :]
                    pool.wait_ge(ln_step, k * 2 + (3 + quad))
                    pool.tensor_tensor(part, part, rs[:, 1:2, :].to_broadcast([P, 4, TOK]), ALU.mult).then_inc(ln_done, 1)

            def splits(k):
                for h in range(2):
                    pool.wait_ge(hi_ready, k * 2 + (3 + h))
                    pool.wait_ge(tok_ready, k * 2 + (3 + h))
                    pool.tensor_tensor(x_tok[h][:, :], x_tok[h][:, :], parts[h][:, 0, :], ALU.subtract).then_inc(rem_ready, 1)
                for h in range(2):
                    pool.wait_ge(mid_ready, k * 2 + (3 + h))
                    pool.tensor_tensor(parts[h][:, 2, :], x_tok[h][:, :], parts[h][:, 1, :], ALU.subtract).then_inc(lo_ready, 1)

            def params_b(k, np_):
                pool.wait_ge(prod_ready, k + 2)
                if has(k, 0, NCH):
                    pool.wait_ge(cw_ready, k * 2 + 2)
                pool.tensor_tensor(cp[:, :], prm[:, 1, :], prod[:, np_, :], ALU.mult).then_inc(cp_ready, 1)

            def one(k, kp):
                np_ = (kp + 1) % 2
                scan, front1, front2 = has(k, 0, NCH - 1), has(k, -2, NCH - 3), has(k, -1, NCH - 2)
                if front2:
                    center(k)
                if has(k, 1, NCH):
                    turn_gate(k - 1, np_, 1)
                if scan:
                    c_weights(k, 1)
                if front2:
                    scale(k)
                if front1:
                    conv(k + 2, 0)
                if front2:
                    splits(k)
                    params_b(k, np_)
                    c_weights(k + 1, 0)
                if front1:
                    conv(k + 2, 1)
                if scan:
                    turn_gate(k, kp, 0)

            chunks(pool, one)


def kernel(x, cond_2048, L0_cond_W_in, L0_cond_W_conv, L0_cond_b_conv, L0_cond_ln_g, L0_cond_ln_b, L0_cond_W_xproj,
           L0_cond_W_dt, L0_cond_b_dt, L0_cond_A_log, L0_cond_D, L0_cond_W_out):
    import ml_dtypes
    import numpy as np
    import concourse.bacc as bacc
    from concourse.bass_utils import run_bass_kernel_spmd

    def tiles(a):
        a = np.asarray(a)
        return np.ascontiguousarray(a.reshape(2, 4, P, -1).transpose(2, 1, 0, 3)).reshape(P, NT, -1)

    w_x = np.asarray(L0_cond_W_xproj)
    bc = tiles(w_x[0:2 * NS].T).reshape(P, NT, 2, NS).transpose(0, 1, 3, 2)
    bc = np.concatenate([bc, np.zeros((P, NT, NS, 1), np.float32)], axis=3)
    dtx = w_x[2 * NS:3 * NS].reshape(NS, 2, 4, P).transpose(0, 2, 1, 3).reshape(NS, NT, P)
    w_dt_t = np.asarray(L0_cond_W_dt).T
    vec = np.concatenate([tiles(L0_cond_W_conv), tiles(L0_cond_b_conv), tiles(L0_cond_ln_g), tiles(L0_cond_ln_b),
                          tiles(L0_cond_D), tiles(np.asarray(cond_2048).T)], axis=2)
    nvec = np.stack([np.tile(np.asarray(L0_cond_A_log), 8), np.tile(np.asarray(L0_cond_b_dt), 8)], axis=1)

    p = np.arange(P)
    batch, half = p // 32, p // 16 % 2
    row = np.arange(XK)
    row_batch, row_q, row_half = row // (4 * XROWS), row // XROWS % 4, row % 2
    sel = ((row_batch[:, None, None] == batch) & (row_half[:, None, None] == half)
           & (row_q[:, None, None] == np.arange(4)[:, None])).astype(ml_dtypes.bfloat16)
    mask = (np.arange(8)[None, :] == (half * 4 + batch)[:, None]).astype(np.float32)
    step_r, step_c, yh, yb = p // 8 % 4, p // 32, p // 4 % 2, p % 4
    perm = (np.arange(P)[None, :] == (yh * 64 + yb * 16 + 4 * step_r + step_c)[:, None]).astype(np.float32)

    arrays = {
        "x_d": np.asarray(x), "vec_d": vec, "w_in_d": np.asarray(L0_cond_W_in).T, "w_out_d": tiles(np.asarray(L0_cond_W_out).T),
        "w_bc_d": np.concatenate([bc, bc], axis=2), "w_dtx_d": dtx,
        "w_dt_d": np.concatenate([w_dt_t, w_dt_t], axis=1), "nvec_d": nvec, "sel_d": sel, "ident_d": np.eye(P, dtype=np.float32),
        "perm_d": perm, "mask_d": mask,
    }
    arrays = {n: np.ascontiguousarray(a) for n, a in arrays.items()}
    nc = bacc.Bacc("TRN2", target_bir_lowering=False, num_devices=1)
    aps = [nc.dram_tensor(n, a.shape, mybir.dt.from_np(a.dtype), kind="ExternalInput").ap() for n, a in arrays.items()]
    out = nc.dram_tensor("out_d", (B, S, DM), F32, kind="ExternalOutput").ap()
    build(nc, *aps, out)
    r = run_bass_kernel_spmd(nc, [arrays], core_ids=[0])
    return r.results[0]["out_d"]
```

```python
from contextlib import ExitStack

import concourse.bass as bass
from concourse import mybir

F32 = mybir.dt.float32
BF16 = mybir.dt.bfloat16
ALU = mybir.AluOpType
ACT = mybir.ActivationFunctionType

P = 128
B, S, DM, DI, NS = 4, 1024, 512, 1024, 16
TAPS = 4
T = 32
NCH = S // T
TOK = B * T
NT = DI // P
KC = DM // P
HALF = DI // 2
GRP = 16
NG = T // GRP
SLOTS = T // 4
RING = 16
XB = 4
SPLIT = 3
XROWS = 2 * SPLIT
XK = XROWS * 4 * B
FIRST, SECOND, LATE = 4, 8, 2
PRM_DMAS = 2 * B
EPS = 1e-5
LIM = 10.0
HIST = TAPS - 1
DMA = 16
XW = 3
V_AT = (3, 4, 6)
PR_AT = (24, 26, 27, 28, 29, 31)

STATS, XT, XR0, PROJ, TOK0, TOK1, XR1, GATE0, GATE1 = range(9)
V_BCONV, V_G, V_B, V_D, V_TEMB, V_ALL = TAPS, TAPS + 1, TAPS + 2, TAPS + 3, TAPS + 4, TAPS + 4 + B


def job(k, place):
    if isinstance(k, int):
        if k == -2:
            return (XT, XR0, XR1).index(place)
        if k == NCH - 2:
            return 9 * k + 12 + (STATS, PROJ, TOK0, TOK1, GATE0, GATE1).index(place)
    return k * 9 + (12 + place)


def job_bank(k, par, place):
    return job(k, place) % 2 if isinstance(k, int) else (par + place) % 2


def build(nc, x, vec, w_in, w_out, w_bc, w_dtx, w_dt, nvec, sel, ident, perm, mask, out):
    with ExitStack() as ctx:
        def sb(name, shape, dt=F32):
            return ctx.enter_context(nc.sbuf_tensor(name, shape, dt))

        def ps(name):
            return ctx.enter_context(nc.psum_tensor(name, [P, 512], F32))

        def sem(name):
            return ctx.enter_context(nc.semaphore(name))

        w_in_s = sb("w_in_s", [P, KC, 2 * DI])
        w_out_s = sb("w_out_s", [P, NT, DM])
        w_proj = sb("w_proj", [P, NT, 32, 3])
        w_dtx_s = sb("w_dtx_s", [NS, NT, P])
        w_dt_s = sb("w_dt_s", [NS, 32])
        vec_s = sb("vec_s", [P, NT, V_ALL])
        nvec_s = sb("nvec_s", [P, 2])
        neg_a = sb("neg_a", [P, 2])
        sel_s = sb("sel_s", [XK, 4, P], BF16)
        ident_s = sb("ident_s", [P, P])
        perm_s = sb("perm_s", [P, P])
        mask_s = sb("mask_s", [P, 8])
        mean_w = sb("mean_w", [P, 32])
        pick_w = sb("pick_w", [P, P])
        ones_w = sb("ones_w", [P, 32])
        zeros = sb("zeros", [P, T])
        conv_bias = sb("conv_bias", [P, NT, B])
        neg_w = sb("neg_w", [P, NT, TAPS])
        w_sum = sb("w_sum", [P, NT, 2])
        x_in = sb("x_in", [P, DM])
        x_t = sb("x_t", [P, 2, KC, TOK])
        taps = [sb(f"taps{q}", [P, 4, TAPS, B, HIST + T]) for q in range(2)]
        cv = [sb(f"cv{q}", [P, 512]) for q in range(2)]
        cv2 = sb("cv2", [P, 512])
        xn = sb("xn", [P, NT, TOK])
        sq = sb("sq", [P, NT, TOK])
        mean = sb("mean", [P, TOK])
        st = sb("st", [P, 2, T])
        st_part = sb("st_part", [P, 2 * TOK])
        rs = sb("rs", [P, 2, T])
        rs_block = sb("rs_block", [P, B, T])
        rstd = sb("rstd", [P, TOK])
        d_xn = [sb(f"d_xn{i}", [P, NT, TOK]) for i in range(2)]
        gate = [sb(f"gate{i}", [P, NT, TOK]) for i in range(2)]
        pr = sb("pr", [P, TOK])
        x_tok = [sb(f"x_tok{h}", [P, 512]) for h in range(2)]
        parts = [sb(f"parts{h}", [P, SPLIT, 512], BF16) for h in range(2)]
        xs = [sb(f"xs{i}", [XK, T // 4, 512], BF16) for i in range(2)]
        prm = sb("prm", [P, 4, T])
        tmp = sb("tmp", [P, 4, T])
        prod = sb("prod", [P, 2, T])
        inv = sb("inv", [P, T])
        cp = sb("cp", [P, T])
        par = [sb(f"par{i}", [P, 3, T]) for i in range(2)]
        cw = [sb(f"cw{g}", [P, 4 * (4 * 32 + 8)]) for g in range(NG)]
        w = sb("w", [P, 512])
        g = sb("g", [P, RING, 512])
        y_row = [sb(f"y_row{i}", [P, 512]) for i in range(2)]
        y_sum = [sb(f"y_sum{i}", [P, 32, GRP]) for i in range(2)]
        yg = [sb(f"yg{i}", [P, NT * B, T]) for i in range(2)]
        x_res = sb("x_res", [P, DM])
        o_sb = [sb(f"o_sb{i}", [P, DM]) for i in range(2)]

        xb = [ps(f"xb{i}") for i in range(XB)]
        y_ps = ps("y_ps")
        a_ps = [ps(f"a_ps{i}") for i in range(2)]
        b_ps = ps("b_ps")

        ident_loaded, first_loaded, second_loaded, late_loaded = (
            sem(n) for n in ("ident_loaded", "first_loaded", "second_loaded", "late_loaded"))
        x_loaded, res_loaded, prm_loaded, xs_loaded, stored = (
            sem(n) for n in ("x_loaded", "res_loaded", "prm_loaded", "xs_loaded", "stored"))
        a_full, a_free, b_full = (sem(n) for n in ("a_full", "a_free", "b_full"))
        xt_ready, silu_done, sq_done = (sem(n) for n in ("xt_ready", "silu_done", "sq_done"))
        taps_free, conv_step, conv_done = ([sem(f"{n}{q}") for q in range(2)] for n in ("taps_free", "conv_step", "conv_done"))
        var_step, ln_step, ln_done, xn_ready, sq_n_done, dxn_ready = (
            sem(n) for n in ("var_step", "ln_step", "ln_done", "xn_ready", "sq_n_done", "dxn_ready"))
        pr_ready, tok_ready, hi_ready, rem_ready, mid_ready, lo_ready = (
            sem(n) for n in ("pr_ready", "tok_ready", "hi_ready", "rem_ready", "mid_ready", "lo_ready"))
        th_ready, a_ready, prod_ready, inv_ready, par_ready, cp_ready, cw_ready = (
            sem(n) for n in ("th_ready", "a_ready", "prod_ready", "inv_ready", "par_ready", "cp_ready", "cw_ready"))
        x_bc, x_used, clipped, y_batch, y_rows, y_turned, y_summed, gated, out_rows, out_ready = (
            sem(n) for n in ("x_bc", "x_used", "clipped", "y_batch", "y_rows", "y_turned", "y_summed", "gated", "out_rows", "out_ready"))
        consts_set, w_dt_made, w_dt_ready, bias_step, bias_ready, cw_zero, a_made = (
            sem(n) for n in ("consts_set", "w_dt_made", "w_dt_ready", "bias_step", "bias_ready", "cw_zero", "a_made"))
        partial_full, partial_ready, block_ready, rstd_full, rstd_out = (
            sem(n) for n in ("partial_full", "partial_ready", "block_ready", "rstd_full", "rstd_out"))
        bn_ready, u_ready, var_ready, std_ready, rstd_ready = (sem(n) for n in ("bn_ready", "u_ready", "var_ready", "std_ready", "rstd_ready"))

        def chan(jh):
            return (jh % 2) * HALF + (jh // 2) * P

        def chunks(eng, one):
            first = 3
            for k in range(-2, first):
                one(k, k % 2)
            turns = (NCH - 3 - first) // 2
            with eng.Fori(0, turns) as i:
                one(i * 2 + first, first % 2)
                one(i * 2 + (first + 1), (first + 1) % 2)
            for k in range(first + 2 * turns, NCH + 1):
                one(k, k % 2)

        def at(k, which):
            return isinstance(k, int) and k == which

        def has(k, lo, hi):
            return lo <= k <= hi if isinstance(k, int) else True

        def conv(eng, two, c, quad):
            eng.wait_ge(a_free, job(c - 2, (XR0, XR1)[quad]) + 1)
            if has(c, 1, NCH):
                eng.wait_ge(silu_done, c * 2 + (quad - 1))
            tp, total, step, n = taps[quad], cv[quad], conv_step[quad], c * 4
            by_tap = "p (a b t) -> p a b t"
            eng.tensor_tensor(total[:, :].rearrange(by_tap, a=4, b=B), tp[:, :, 0, :, 0:T], tp[:, :, 1, :, 1:1 + T], ALU.add).then_inc(step, 1)
            eng.tensor_tensor(two[:, :].rearrange(by_tap, a=4, b=B), tp[:, :, 2, :, 2:2 + T], tp[:, :, 3, :, 3:3 + T], ALU.add).then_inc(step, 1)
            eng.wait_ge(step, n + 2)
            eng.tensor_tensor(total[:, :], total[:, :], two[:, :], ALU.add).then_inc(step, 1)
            eng.tensor_copy(tp[:, :, :, :, 0:HIST].rearrange("p a k b t -> p (a k b) t"),
                            tp[:, :, :, :, T:T + HIST].rearrange("p a k b t -> p (a k b) t")).then_inc(taps_free[quad], 1)
            eng.wait_ge(step, n + 3)
            rows = total[:, :].rearrange("p (a t) -> p a t", t=T)
            eng.tensor_tensor(rows, rows, conv_bias[:, 4 * quad:4 * quad + 4, :].rearrange("p a b -> p (a b)").unsqueeze(2)
                              .to_broadcast([P, 16, T]), ALU.add).then_inc(step, 1)
            eng.wait_ge(step, n + 4)
            eng.sem_inc(conv_done[quad], 1)

        block = ctx.enter_context(nc.Block())

        @block.sync
        def _(sp):
            w_rows = w_in.rearrange("(c p) n -> p c n", p=P)
            quad_cols = [[slice(HALF * h + 2 * P * quad, HALF * h + 2 * P * (quad + 1)) for h in range(2)] for quad in range(2)]
            sp.dma_start(x_in[:, :], x[:, 0:T, :]).then_inc(x_loaded, DMA)
            sp.dma_start(ident_s[:, :], ident).then_inc(ident_loaded, DMA)
            for dst, src in ((vec_s[:, :, :], vec), (nvec_s[:, :], nvec)):
                sp.dma_start(dst, src).then_inc(first_loaded, DMA)
            for cols in quad_cols[0]:
                sp.dma_start(w_in_s[:, :, cols], w_rows[:, :, cols]).then_inc(first_loaded, DMA)
            for cols in quad_cols[1]:
                sp.dma_start(w_in_s[:, :, cols], w_rows[:, :, cols]).then_inc(second_loaded, DMA)
            for dst, src in ((w_proj[:, :, :, :], w_bc), (w_dtx_s[:, :, :], w_dtx), (w_dt_s[:, :], w_dt),
                             (sel_s[:, :, :], sel), (perm_s[:, :], perm), (mask_s[:, :], mask)):
                sp.dma_start(dst, src).then_inc(second_loaded, DMA)
            for dst, src in ((w_in_s[:, :, DI:2 * DI], w_rows[:, :, DI:2 * DI]), (w_out_s[:, :, :], w_out)):
                sp.dma_start(dst, src).then_inc(late_loaded, DMA)

            def one(k, kp):
                np_ = (kp + 1) % 2

                def val(v):
                    return v if isinstance(v, int) else sp.snap(v)

                k0, k1, k2, steps = val(k), val(k + 1), val(k + 2), val(k * T)
                lo_h = [val(k * 2 + (3 + h)) for h in range(2)]
                turned = val(job(k, XT) + 1) if has(k, -2, NCH - 3) else None
                at_prev, at_this, at_next = val((k - 1) * T), val(k * T), val((k + 3) * T)
                if has(k, -2, NCH - 4):
                    sp.wait_ge(a_full, turned)
                    sp.dma_start(x_in[:, :], x[:, bass.ds(at_next, T), :]).then_inc(x_loaded, DMA)
                if has(k, -1, NCH - 2):
                    sp.wait_ge(pr_ready, k2)
                    for b in range(B):
                        sp.dma_start(prm[32 * b:32 * b + 32, 0:3, :], pr[0:96, T * b:T * b + T]).then_inc(prm_loaded, DMA)
                        sp.dma_start(prm[32 * b:32 * b + 32, 3, :], pr[96:P, T * b:T * b + T]).then_inc(prm_loaded, DMA)
                    if has(k, 1, NCH):
                        sp.wait_ge(x_bc, steps)
                    for h in range(2):
                        sp.wait_ge(lo_ready, lo_h[h])
                        wide = xs[np_][:, :, :].ap[0][0]
                        for part in range(SPLIT):
                            rows = bass.AP(tensor=xs[np_][:, :, :].tensor, offset=(2 * part + h) * wide,
                                           ap=[[XROWS * wide, 4 * B], [512, T // 4], [1, 512]])
                            sp.dma_start(rows, parts[h][:, part, :]).then_inc(xs_loaded, DMA)
                if has(k, 1, NCH):
                    sp.wait_ge(out_ready, k0)
                    sp.dma_start(out[:, bass.ds(at_prev, T), :], o_sb[np_][:, :]).then_inc(stored, DMA)
                if has(k, 0, NCH - 1):
                    sp.dma_start(x_res[:, :], x[:, bass.ds(at_this, T), :]).then_inc(res_loaded, DMA)

            chunks(sp, one)
            sp.wait_ge(stored, DMA * NCH)

        @block.tensor
        def _(pe):
            def open_job(k, place):
                n = job(k, place)
                if not isinstance(n, int) or n >= 2:
                    pe.wait_ge(a_free, n - 1)

            def in_quad(k, kp, chunk_par, place, quad, col0, s):
                if s == 0:
                    open_job(k, place)
                jh = 4 * quad + s
                for c in range(KC):
                    mm = pe.matmul(a_ps[job_bank(k, kp, place)][:, TOK * s:TOK * s + TOK],
                                   w_in_s[:, c, col0 + chan(jh):col0 + chan(jh) + P],
                                   x_t[:, chunk_par, c, :], start=(c == 0), stop=(c == KC - 1))
                if s == 3:
                    mm.then_inc(a_full, 1)

            def x_transpose(k, kp):
                open_job(k, XT)
                if at(k, -2):
                    pe.wait_ge(ident_loaded, DMA)
                pe.wait_ge(x_loaded, (k + 3) * DMA)
                for c in range(KC):
                    mm = pe.transpose(a_ps[job_bank(k, kp, XT)][:, TOK * c:TOK * c + TOK],
                                      x_in[:, P * c:P * c + P], ident_s[:, :])
                mm.then_inc(a_full, 1)

            def bring_x(k, kp, t):
                q = t // (T // 4)
                if not (at(k, 0) and t < XB):
                    pe.wait_ge(x_used, k * T + (t - XB + 1))
                pe.matmul(xb[t % XB][:, :], sel_s[:, q, :], xs[kp][:, t % (T // 4), :],
                          start=True, stop=True).then_inc(x_bc, 1)

            def contract(k, slot):
                grp, r = slot // 4, slot % 4
                pe.wait_ge(clipped, k * T + 4 * slot + 4)
                if r == 0:
                    pe.wait_ge(cw_ready, k * 2 + (grp + 1))
                    if not (at(k, 0) and grp == 0):
                        pe.wait_ge(y_rows, k * 2 + grp)
                for c in range(4):
                    t = 4 * slot + c
                    s = 4 * r + c
                    mm = pe.matmul(y_ps[32 * c:32 * c + 32, :], cw[grp][:, 32 * s:32 * s + 32], g[:, t % RING, :],
                                   start=(r == 0), stop=(r == 3), tile_position=(0, 32 * c))
                mm.then_inc(y_batch, 1)

            def y_turn(k, grp):
                pe.wait_ge(y_rows, k * 2 + (grp + 1))
                if grp == 1:
                    pe.wait_ge(y_turned, k * 2 + 1)
                elif not at(k, 0):
                    pe.wait_ge(out_rows, k)
                for j in range(4):
                    mm = pe.transpose(b_ps[:, P * j:P * j + P], y_row[grp][:, P * j:P * j + P], perm_s[:, :])
                mm.then_inc(b_full, 1)

            def out_part(k, kp, quarter):
                if quarter == 0:
                    if has(k, 0, NCH - 3):
                        pe.wait_ge(rstd_out, k + 3)
                    pe.wait_ge(gated, k * 2 + 2)
                jh = quarter
                mm = pe.matmul(b_ps[:, :], yg[kp][:, B * jh:B * jh + B, :], w_out_s[:, jh, :],
                               start=(jh == 0), stop=(jh == NT - 1))
                if jh == NT - 1:
                    mm.then_inc(b_full, 1)

            def stats_partial(k, kp):
                open_job(k, STATS)
                if at(k, -1):
                    pe.wait_ge(consts_set, 1)
                pe.wait_ge(sq_done, k * 2 + 4)
                for part, src in ((0, xn), (1, sq)):
                    for jh in range(NT):
                        c = jh % 4
                        mm = pe.matmul(a_ps[job_bank(k, kp, STATS)][32 * c:32 * c + 32, TOK * part:TOK * part + TOK],
                                       mean_w[:, :], src[:, jh, :], start=(jh < 4), stop=(jh >= 4), tile_position=(0, 32 * c))
                mm.then_inc(partial_full, 1)

            def stats_total(k, kp):
                pe.wait_ge(partial_ready, k + 2)
                bank = a_ps[job_bank(k, kp, STATS)]
                pe.matmul(bank[:, 2 * TOK:3 * TOK], pick_w[:, :], st_part[:, 0:TOK], start=True, stop=True)
                for b in range(B):
                    mm = pe.matmul(bank[32 * b:32 * b + 32, 3 * TOK:3 * TOK + 2 * T], pick_w[:, 0:32],
                                   st_part[:, :].rearrange("p (v b t) -> p b v t", v=2, b=B)[:, b, :, :],
                                   start=True, stop=True, tile_position=(0, 32 * b))
                mm.then_inc(a_full, 1)

            def rstd_total(k):
                pe.wait_ge(block_ready, k + 2)
                if at(k, -1):
                    pe.wait_ge(w_dt_ready, 1)
                if has(k, 1, NCH):
                    pe.wait_ge(y_turned, k * 2)
                pe.matmul(b_ps[:, 0:TOK], pick_w[:, :], rs_block[:, :, :].rearrange("p b t -> p (b t)"),
                          start=True, stop=True).then_inc(rstd_full, 1)

            def project(k, kp, part):
                if part == 0:
                    open_job(k, PROJ)
                    pe.wait_ge(sq_n_done, k * 2 + 4)
                for jh in range(4 * part, 4 * part + 4):
                    for kind in range(4):
                        lhs = w_cols[:, jh, 32 * kind:32 * kind + 32] if kind < 3 else ones_w[:, :]
                        mm = pe.matmul(a_ps[job_bank(k, kp, PROJ)][32 * kind:32 * kind + 32, 0:TOK], lhs,
                                       (xn if kind < 3 else sq)[:, jh, :], start=(jh == 0), stop=(jh == NT - 1),
                                       tile_position=(0, 32 * kind))
                if part == 1:
                    mm.then_inc(a_full, 1)

            w_cols = w_proj[:, :, :, :].rearrange("p a s k -> p a (s k)")

            def to_tokens(k, kp, h):
                place = (TOK0, TOK1)[h]
                open_job(k, place)
                for j in range(4):
                    mm = pe.transpose(a_ps[job_bank(k, kp, place)][:, P * j:P * j + P], xn[:, 2 * j + h, :], ident_s[:, :])
                mm.then_inc(a_full, 1)

            def one(k, kp):
                np_ = (kp + 1) % 2
                scan, front1, front2 = has(k, 0, NCH - 1), has(k, -2, NCH - 3), has(k, -1, NCH - 2)
                back = has(k, 1, NCH)
                for slot in range(SLOTS):
                    for s in range(4):
                        t = 4 * slot + s
                        if scan:
                            if t + XB - 1 < T:
                                bring_x(k, kp, t + XB - 1)
                        if t + XB - 1 >= T and has(k, -1, NCH - 2):
                            if t + XB - 1 == T:
                                pe.wait_ge(xs_loaded, (k + 2) * (2 * SPLIT * DMA))
                            bring_x(k + 1, np_, t + XB - 1 - T)
                        if s == 1:
                            if slot == 0 and back:
                                contract(k - 1, SLOTS - 1)
                            if slot > 0 and scan:
                                contract(k, slot - 1)
                        if slot == 0 and s == 0 and front2:
                            stats_partial(k, kp)
                        if slot == 0 and s == 2 and front2:
                            stats_total(k, kp)
                        if slot == 0 and s == 3 and front1:
                            x_transpose(k, kp)
                        if slot == 1 and s == 0 and back:
                            y_turn(k - 1, 1)
                        if slot == 1 and front1:
                            if s == 0:
                                pe.wait_ge(xt_ready, k + 3)
                                if at(k, -2):
                                    pe.wait_ge(first_loaded, FIRST * DMA)
                            in_quad(k, kp, kp, XR0, 0, 0, s)
                        if slot == 2 and s == 0 and front2:
                            rstd_total(k)
                        if slot in (2, 5) and back:
                            out_part(k - 1, np_, 4 * (slot == 5) + s)
                        if slot == 3 and s in (1, 2) and front2:
                            project(k, kp, s - 1)
                        if slot == 3 and s >= 2 and front2:
                            to_tokens(k, kp, s - 2)
                        if slot == 4 and s == 0 and at(k, -2):
                            pe.wait_ge(second_loaded, SECOND * DMA)
                        if slot == 5 and s == 0 and at(k, -2):
                            for jh in range(NT):
                                mm = pe.matmul(b_ps[:, 32 * jh:32 * jh + 32], w_dtx_s[:, jh, :], w_dt_s[:, :], start=True, stop=True)
                            mm.then_inc(w_dt_made, 1)
                        if slot == 6 and s == 0 and at(k, -1):
                            pe.wait_ge(late_loaded, LATE * DMA)
                        if slot == 4 and front1:
                            in_quad(k, kp, kp, XR1, 1, 0, s)
                        if slot == 6 and front2:
                            in_quad(k, kp, np_, GATE0, 0, DI, s)
                        if slot == 6 and s == 3 and scan:
                            y_turn(k, 0)
                        if slot == 7 and front2:
                            in_quad(k, kp, np_, GATE1, 1, DI, s)

            chunks(pe, one)

        @block.scalar
        def _(act):
            def take(k, kp, place):
                act.wait_ge(a_full, job(k, place) + 1)
                return a_ps[job_bank(k, kp, place)]

            def start():
                act.wait_ge(first_loaded, FIRST * DMA)
                act.activation(neg_a[:, 0:1], nvec_s[:, 0:1], ACT.Tanh).then_inc(a_made, 1)
                act.wait_ge(a_made, 1)
                act.activation(neg_a[:, 1:2], neg_a[:, 0:1], ACT.Copy, scale=-0.01).then_inc(a_made, 1)
                act.wait_ge(a_made, 2)

            def gates(k, kp, place, quad, chunk_par):
                src = take(k, kp, place)
                if has(k, 1, NCH):
                    act.wait_ge(gated, k * 2)
                act.activation(gate[chunk_par][:, 4 * quad:4 * quad + 4, :].rearrange("p a b -> p (a b)"), src[:, :],
                               ACT.Silu).then_inc(a_free, 1)

            def rows_out(k, grp):
                act.wait_ge(y_batch, k * SLOTS + 4 * (grp + 1))
                if has(k, 1, NCH):
                    act.wait_ge(b_full, k * 3 - (2 if grp == 0 else 1))
                act.activation(y_row[grp][:, :], y_ps[:, :], ACT.Copy).then_inc(y_rows, 1)

            def turned_out(k, grp):
                act.wait_ge(b_full, k * 3 + (grp + 1))
                if has(k, 1, NCH):
                    act.wait_ge(gated, k * 2 + (grp - 1))
                act.activation(y_sum[grp][:, :, :].rearrange("p a t -> p (a t)"), b_ps[:, :], ACT.Copy).then_inc(y_turned, 1)

            def product_out(k, kp):
                act.wait_ge(b_full, k * 3 + 3)
                if has(k, 1, NCH):
                    act.wait_ge(stored, k * DMA)
                act.activation(o_sb[kp][:, :], b_ps[:, :], ACT.Copy).then_inc(out_rows, 1)

            def silu(c, quad):
                act.wait_ge(conv_done[quad], c + 1)
                part = xn[:, 4 * quad:4 * quad + 4, :].rearrange("p a b -> p (a b)")
                act.activation(part, cv[quad][:, :], ACT.Silu).then_inc(silu_done, 1)
                act.wait_ge(silu_done, c * 2 + (quad + 1))
                act.activation(sq[:, 4 * quad:4 * quad + 4, :].rearrange("p a b -> p (a b)"), part,
                               ACT.Square).then_inc(sq_done, 1)

            def times_d(k, np_):
                if has(k, 1, NCH):
                    act.wait_ge(y_summed, k * 2)
                for jh in range(NT):
                    last = act.activation(d_xn[np_][:, jh, :], xn[:, jh, :], ACT.Copy, scale=vec_s[:, jh, V_D:V_D + 1])
                last.then_inc(dxn_ready, 1)

            def tap_products(k, kp, quad):
                src = take(k, kp, (XR0, XR1)[quad])
                act.wait_ge(taps_free[quad], k + 3)
                for d in range(4):
                    for tap in range(TAPS):
                        last = act.activation(taps[quad][:, d, tap, :, HIST:HIST + T],
                                              src[:, TOK * d:TOK * d + TOK].rearrange("p (b t) -> p b t", b=B),
                                              ACT.Copy, scale=vec_s[:, 4 * quad + d, tap:tap + 1])
                last.then_inc(a_free, 1)

            def one(k, kp):
                np_ = (kp + 1) % 2
                scan, front1, front2 = has(k, 0, NCH - 1), has(k, -2, NCH - 3), has(k, -1, NCH - 2)
                back = has(k, 1, NCH)
                if at(k, -1):
                    start()
                if front2:
                    act.wait_ge(partial_full, k + 2)
                    bank = a_ps[job_bank(k, kp, STATS)]
                    act.activation(st_part[:, :], bank[:, 0:2 * TOK], ACT.Copy).then_inc(partial_ready, 1)
                if back:
                    rows_out(k - 1, 1)
                if front2:
                    src = take(k, kp, STATS)
                    act.activation(mean[:, :], src[:, 2 * TOK:3 * TOK], ACT.Copy)
                    act.activation(st[:, 0, :], src[:, 3 * TOK:3 * TOK + T], ACT.Square)
                    act.activation(st[:, 1, :], src[:, 3 * TOK + T:3 * TOK + 2 * T], ACT.Copy, bias=EPS).then_inc(a_free, 1)
                if front1:
                    src = take(k, kp, XT)
                    act.activation(x_t[:, kp, :, :].rearrange("p a b -> p (a b)"), src[:, :], ACT.Copy).then_inc(xt_ready, 1)
                    act.wait_ge(xt_ready, k + 3)
                    act.sem_inc(a_free, 1)
                if front2:
                    act.wait_ge(var_ready, k + 2)
                    act.activation(rs[:, 1, :], rs[:, 0, :], ACT.Sqrt).then_inc(std_ready, 1)
                if back:
                    turned_out(k - 1, 1)
                if front2:
                    act.wait_ge(rstd_ready, k + 2)
                    for b in range(B):
                        last = act.activation(rs_block[32 * b:32 * b + 32, b, :], rs[32 * b:32 * b + 32, 1, :], ACT.Copy)
                    last.then_inc(block_ready, 1)
                    act.wait_ge(rstd_full, k + 2)
                    act.activation(rstd[:, :], b_ps[:, 0:TOK], ACT.Copy).then_inc(rstd_out, 1)
                    for quad in range(2):
                        act.wait_ge(ln_done, k * 2 + (3 + quad))
                        for jh in range(4 * quad, 4 * quad + 4):
                            last = act.activation(xn[:, jh, :], xn[:, jh, :], ACT.Identity, bias=vec_s[:, jh, V_B:V_B + 1],
                                                  scale=vec_s[:, jh, V_G:V_G + 1])
                        last.then_inc(xn_ready, 1)
                        act.wait_ge(xn_ready, k * 2 + (3 + quad))
                        act.activation(sq[:, 4 * quad:4 * quad + 4, :].rearrange("p a b -> p (a b)"),
                                       xn[:, 4 * quad:4 * quad + 4, :].rearrange("p a b -> p (a b)"),
                                       ACT.Square).then_inc(sq_n_done, 1)
                if front1:
                    tap_products(k, kp, 0)
                if front2:
                    src = take(k, kp, PROJ)
                    if has(k, 0, NCH):
                        act.wait_ge(prm_loaded, (k + 1) * (PRM_DMAS * DMA))
                    act.activation(pr[:, :], src[:, 0:TOK], ACT.Copy).then_inc(pr_ready, 1)
                    act.wait_ge(pr_ready, k + 2)
                    act.sem_inc(a_free, 1)
                    for h in range(2):
                        src = take(k, kp, (TOK0, TOK1)[h])
                        if has(k, 0, NCH):
                            act.wait_ge(lo_ready, k * 2 + (h + 1))
                            act.wait_ge(xs_loaded, (k + 1) * (2 * SPLIT * DMA))
                        act.activation(x_tok[h][:, :], src[:, :], ACT.Copy).then_inc(tok_ready, 1)
                        act.activation(parts[h][:, 0, :], src[:, :], ACT.Copy).then_inc(hi_ready, 1)
                        act.wait_ge(hi_ready, k * 2 + (3 + h))
                        act.wait_ge(tok_ready, k * 2 + (3 + h))
                        act.sem_inc(a_free, 1)
                    times_d(k, np_)
                if scan:
                    rows_out(k, 0)
                if front2:
                    for h in range(2):
                        act.wait_ge(rem_ready, k * 2 + (3 + h))
                        act.activation(parts[h][:, 1, :], x_tok[h][:, :], ACT.Copy).then_inc(mid_ready, 1)
                    act.wait_ge(prm_loaded, (k + 2) * (PRM_DMAS * DMA))
                    act.activation(tmp[:, 2, :], prm[:, 2, :], ACT.Tanh, bias=nvec_s[:, 1:2]).then_inc(th_ready, 1)
                    act.wait_ge(th_ready, k + 2)
                    act.activation(tmp[:, 3, :], tmp[:, 2, :], ACT.Copy, scale=neg_a[:, 1:2], bias=1.0).then_inc(a_ready, 1)
                    act.activation(tmp[:, 1, :], prm[:, 3, :], ACT.Sqrt).then_inc(bn_ready, 1)
                if front1:
                    tap_products(k, kp, 1)
                if at(k, -1):
                    gates(k, kp, GATE0, 0, np_)
                if back:
                    product_out(k - 1, np_)
                if front1:
                    silu(k + 2, 0)
                if scan:
                    turned_out(k, 0)
                if front1:
                    silu(k + 2, 1)
                if front2:
                    if not at(k, -1):
                        gates(k, kp, GATE0, 0, np_)
                    gates(k, kp, GATE1, 1, np_)

            chunks(act, one)

        @block.vector
        def _(dve):
            dve.memset(pick_w[:, :], 0.0).then_inc(bias_step, 1)
            dve.wait_ge(bias_step, 1)
            for c in range(4):
                dve.memset(pick_w[32 * c:32 * c + 1, :], 1.0)
            dve.memset(mean_w[:, :], 1.0 / DI)
            dve.memset(zeros[:, :], 0.0)
            dve.memset(rs_block[:, :, :], 0.0)
            dve.memset(g[:, RING - 1, :], 0.0)
            dve.memset(ones_w[:, :], 1.0).then_inc(consts_set, 1)
            dve.wait_ge(first_loaded, FIRST * DMA)
            w_v = vec_s[:, :, 0:TAPS]
            dve.tensor_scalar(neg_w[:, :, :], w_v, -1.0, None, ALU.mult).then_inc(bias_step, 1)
            dve.tensor_tensor(w_sum[:, :, :], w_v[:, :, 0:2], w_v[:, :, 2:4], ALU.add).then_inc(bias_step, 1)
            dve.wait_ge(bias_step, 3)
            for quad in range(2):
                for d in range(4):
                    jh = 4 * quad + d
                    for b in range(B):
                        last = dve.tensor_scalar(taps[quad][:, d, :, b, 0:HIST],
                                                 neg_w[:, jh, :].unsqueeze(2).to_broadcast([P, TAPS, HIST]),
                                                 vec_s[:, jh, V_TEMB + b:V_TEMB + b + 1], None, ALU.mult)
                last.then_inc(taps_free[quad], 1)
            dve.tensor_tensor(w_sum[:, :, 0:1], w_sum[:, :, 0:1], w_sum[:, :, 1:2], ALU.add).then_inc(bias_step, 1)
            dve.wait_ge(bias_step, 4)
            temb = vec_s[:, :, V_TEMB:V_TEMB + B]
            dve.tensor_tensor(conv_bias[:, :, :], temb, w_sum[:, :, 0:1].to_broadcast([P, NT, B]), ALU.mult).then_inc(bias_step, 1)
            dve.wait_ge(bias_step, 5)
            dve.tensor_tensor(conv_bias[:, :, :], conv_bias[:, :, :], vec_s[:, :, V_BCONV:V_BCONV + 1].to_broadcast([P, NT, B]),
                              ALU.add).then_inc(bias_ready, 1)

            def variance(k, piece):
                if piece == 0:
                    dve.wait_ge(a_free, job(k, STATS) + 1)
                    dve.tensor_tensor(rs[:, 0, :], st[:, 1, :], st[:, 0, :], ALU.subtract).then_inc(var_step, 1)
                elif piece == 1:
                    dve.wait_ge(var_step, k + 2)
                    dve.tensor_scalar(rs[:, 0, :], rs[:, 0, :], EPS, None, ALU.max).then_inc(var_ready, 1)
                else:
                    dve.wait_ge(std_ready, k + 2)
                    dve.reciprocal(rs[:, 1, :], rs[:, 1, :]).then_inc(rstd_ready, 1)

            def run_prod(k, kp, piece):
                if piece == 0:
                    dve.wait_ge(a_ready, k + 1)
                    first = at(k, 0)
                    dve.tensor_tensor_scan(prod[:, kp, :], tmp[:, 3, :], zeros[:, :],
                                           1.0 if first else prod[:, (kp + 1) % 2, T - 1:T], ALU.mult, ALU.add).then_inc(prod_ready, 1)
                elif piece == 1:
                    dve.wait_ge(prod_ready, k + 1)
                    dve.reciprocal(inv[:, :], prod[:, kp, :]).then_inc(inv_ready, 1)
                elif piece == 2:
                    dve.wait_ge(bn_ready, k + 1)
                    dve.scalar_tensor_tensor(out=tmp[:, 0, :], in0=tmp[:, 1, :], scalar=1.0, in1=prm[:, 0, :],
                                             op0=ALU.min, op1=ALU.mult).then_inc(u_ready, 1)
                elif piece == 3:
                    dve.wait_ge(inv_ready, k + 1)
                    dve.tensor_scalar(par[kp][:, 1, :], inv[:, :], LIM, None, ALU.mult)
                elif piece == 4:
                    dve.tensor_scalar(par[kp][:, 2, :], inv[:, :], -LIM, None, ALU.mult)
                else:
                    dve.wait_ge(u_ready, k + 1)
                    dve.tensor_tensor(par[kp][:, 0, :], tmp[:, 0, :], inv[:, :], ALU.mult).then_inc(par_ready, 1)

            def one(k, kp):
                np_ = (kp + 1) % 2
                if not has(k, 0, NCH - 1):
                    if at(k, -2):
                        dve.wait_ge(second_loaded, SECOND * DMA)
                        dve.wait_ge(w_dt_made, 1)
                        dve.tensor_copy(w_proj[:, :, :, 2], b_ps[:, 0:32 * NT].rearrange("p (a b) -> p a b", b=32)).then_inc(w_dt_ready, 1)
                        dve.wait_ge(bias_ready, 1)
                        conv(dve, w, 0, 1)
                    if at(k, -1):
                        for piece in range(3):
                            variance(k, piece)
                        conv(dve, w, 1, 0)
                        for piece in range(6):
                            run_prod(0, 0, piece)
                    return
                first = at(k, 0)
                for t in range(T):
                    if first and t < 2 * XW:
                        dve.wait_ge(x_bc, t + 1)
                    elif t % XW == 0:
                        dve.wait_ge(x_bc, k * T + min(t + XW, T))
                    if first and t == 0:
                        dve.wait_ge(par_ready, k + 1)
                    if not (first and t == 0):
                        dve.wait_ge(clipped, k * T + t)
                    dve.scalar_tensor_tensor(out=w[:, :], in0=xb[t % XB][:, :], scalar=par[kp][:, 0, t:t + 1],
                                             in1=g[:, (t - 1) % RING, :], op0=ALU.mult, op1=ALU.add).then_inc(x_used, 1)
                    if has(k, 0, NCH - 2):
                        if t in V_AT:
                            variance(k, V_AT.index(t))
                        if t in PR_AT:
                            run_prod(k + 1, np_, PR_AT.index(t))
                    dve.wait_ge(x_used, k * T + (t + 1))
                    dve.tensor_scalar(g[:, t % RING, :], w[:, :], par[kp][:, 1, t:t + 1], par[kp][:, 2, t:t + 1],
                                      ALU.min, ALU.max).then_inc(clipped, 1)

            chunks(dve, one)

        @block.gpsimd
        def _(pool):
            for i in range(NG):
                last = pool.memset(cw[i][:, :], 0.0)
            last.then_inc(cw_zero, 1)
            pool.wait_ge(cw_zero, 1)
            pool.wait_ge(bias_ready, 1)
            pool.wait_ge(second_loaded, SECOND * DMA)

            def turn_gate(k, kp, grp):
                pool.wait_ge(y_turned, k * 2 + (grp + 1))
                sl = slice(GRP * grp, GRP * grp + GRP)
                if grp == 0:
                    pool.wait_ge(dxn_ready, k + 1)
                pool.tensor_tensor(y_sum[grp][:, :, :], y_sum[grp][:, :, :],
                                   d_xn[kp][:, :, :].rearrange("p a (b t) -> p (a b) t", t=T)[:, :, sl], ALU.add).then_inc(y_summed, 1)
                pool.wait_ge(y_summed, k * 2 + (grp + 1))
                pool.wait_ge(a_free, job(k - 1, GATE1) + 1)
                if has(k, 2, NCH):
                    pool.wait_ge(b_full, k * 3 - 3)
                pool.tensor_tensor(yg[kp][:, :, sl], y_sum[grp][:, :, :],
                                   gate[kp][:, :, :].rearrange("p a (b t) -> p (a b) t", t=T)[:, :, sl],
                                   ALU.mult).then_inc(gated, 1)

            def add_x(k, kp):
                pool.wait_ge(out_rows, k + 1)
                pool.wait_ge(res_loaded, (k + 1) * DMA)
                pool.tensor_tensor(o_sb[kp][:, :], o_sb[kp][:, :], x_res[:, :], ALU.add).then_inc(out_ready, 1)

            def c_weights(k, grp):
                if grp == 0:
                    pool.wait_ge(cp_ready, k + 1)
                if has(k, 1, NCH):
                    pool.wait_ge(y_batch, k * SLOTS - (4 if grp == 0 else 0))
                dst = cw[grp][:, :].rearrange("p (r v) -> p r v", r=4)[:, :, 0:4 * 32]
                dst = dst.rearrange("p r (c m) -> p r c m", c=4)[:, :, :, 0:8]
                src = cp[:, GRP * grp:GRP * grp + GRP].rearrange("p (r c) -> p r c", c=4).unsqueeze(3).to_broadcast([P, 4, 4, 8])
                m = mask_s[:, :].unsqueeze(1).unsqueeze(1).to_broadcast([P, 4, 4, 8])
                pool.tensor_tensor(dst, src, m, ALU.mult).then_inc(cw_ready, 1)

            def center(k):
                pool.wait_ge(a_free, job(k, STATS) + 1)
                for quad in range(2):
                    part = xn[:, 4 * quad:4 * quad + 4, :]
                    pool.tensor_tensor(part, part, mean[:, :].unsqueeze(1).to_broadcast([P, 4, TOK]), ALU.subtract).then_inc(ln_step, 1)

            def scale(k):
                pool.wait_ge(rstd_out, k + 2)
                for quad in range(2):
                    part = xn[:, 4 * quad:4 * quad + 4, :]
                    pool.wait_ge(ln_step, k * 2 + (3 + quad))
                    pool.tensor_tensor(part, part, rstd[:, :].unsqueeze(1).to_broadcast([P, 4, TOK]), ALU.mult).then_inc(ln_done, 1)

            def splits(k):
                for h in range(2):
                    pool.wait_ge(hi_ready, k * 2 + (3 + h))
                    pool.wait_ge(tok_ready, k * 2 + (3 + h))
                    pool.tensor_tensor(x_tok[h][:, :], x_tok[h][:, :], parts[h][:, 0, :], ALU.subtract).then_inc(rem_ready, 1)
                for h in range(2):
                    pool.wait_ge(mid_ready, k * 2 + (3 + h))
                    pool.tensor_tensor(parts[h][:, 2, :], x_tok[h][:, :], parts[h][:, 1, :], ALU.subtract).then_inc(lo_ready, 1)

            def c_times_p(k, np_):
                pool.wait_ge(prod_ready, k + 2)
                if has(k, 0, NCH):
                    pool.wait_ge(cw_ready, k * 2 + 2)
                pool.tensor_tensor(cp[:, :], prm[:, 1, :], prod[:, np_, :], ALU.mult).then_inc(cp_ready, 1)

            def one(k, kp):
                np_ = (kp + 1) % 2
                scan, front1, front2 = has(k, 0, NCH - 1), has(k, -2, NCH - 3), has(k, -1, NCH - 2)
                if front2:
                    center(k)
                if has(k, 1, NCH):
                    turn_gate(k - 1, np_, 1)
                if scan:
                    c_weights(k, 1)
                if front2:
                    scale(k)
                if has(k, 0, NCH - 3):
                    conv(pool, cv2, k + 2, 0)
                if at(k, -2):
                    conv(pool, cv2, 0, 0)
                if front2:
                    splits(k)
                    c_times_p(k, np_)
                    c_weights(k + 1, 0)
                if has(k, -1, NCH - 3):
                    conv(pool, cv2, k + 2, 1)
                if has(k, 1, NCH):
                    add_x(k - 1, np_)
                if scan:
                    turn_gate(k, kp, 0)

            chunks(pool, one)


def kernel(x, cond_2048, L0_cond_W_in, L0_cond_W_conv, L0_cond_b_conv, L0_cond_ln_g, L0_cond_ln_b, L0_cond_W_xproj,
           L0_cond_W_dt, L0_cond_b_dt, L0_cond_A_log, L0_cond_D, L0_cond_W_out):
    import ml_dtypes
    import numpy as np
    import concourse.bacc as bacc
    from concourse.bass_utils import run_bass_kernel_spmd

    def tiles(a):
        a = np.asarray(a)
        return np.ascontiguousarray(a.reshape(2, 4, P, -1).transpose(2, 1, 0, 3)).reshape(P, NT, -1)

    w_x = np.asarray(L0_cond_W_xproj)
    bc = tiles(w_x[0:2 * NS].T).reshape(P, NT, 2, NS).transpose(0, 1, 3, 2)
    bc = np.concatenate([bc, np.zeros((P, NT, NS, 1), np.float32)], axis=3)
    dtx = w_x[2 * NS:3 * NS].reshape(NS, 2, 4, P).transpose(0, 2, 1, 3).reshape(NS, NT, P)
    w_dt_t = np.asarray(L0_cond_W_dt).T
    vec = np.concatenate([tiles(L0_cond_W_conv), tiles(L0_cond_b_conv), tiles(L0_cond_ln_g), tiles(L0_cond_ln_b),
                          tiles(L0_cond_D), tiles(np.asarray(cond_2048).T)], axis=2)
    nvec = np.stack([np.tile(np.asarray(L0_cond_A_log), 8), np.tile(np.asarray(L0_cond_b_dt), 8)], axis=1)

    p = np.arange(P)
    batch, half = p // 32, p // 16 % 2
    row = np.arange(XK)
    row_batch, row_q, row_half = row // (4 * XROWS), row // XROWS % 4, row % 2
    sel = ((row_batch[:, None, None] == batch) & (row_half[:, None, None] == half)
           & (row_q[:, None, None] == np.arange(4)[:, None])).astype(ml_dtypes.bfloat16)
    mask = (np.arange(8)[None, :] == (half * 4 + batch)[:, None]).astype(np.float32)
    step_r, step_c, yh, yb = p // 8 % 4, p // 32, p // 4 % 2, p % 4
    perm = (np.arange(P)[None, :] == (yh * 64 + yb * 16 + 4 * step_r + step_c)[:, None]).astype(np.float32)

    arrays = {
        "x_d": np.asarray(x), "vec_d": vec, "w_in_d": np.asarray(L0_cond_W_in).T, "w_out_d": tiles(np.asarray(L0_cond_W_out).T),
        "w_bc_d": np.concatenate([bc, bc], axis=2), "w_dtx_d": dtx,
        "w_dt_d": np.concatenate([w_dt_t, w_dt_t], axis=1), "nvec_d": nvec, "sel_d": sel, "ident_d": np.eye(P, dtype=np.float32),
        "perm_d": perm, "mask_d": mask,
    }
    arrays = {n: np.ascontiguousarray(a) for n, a in arrays.items()}
    nc = bacc.Bacc("TRN2", target_bir_lowering=False, num_devices=1)
    aps = [nc.dram_tensor(n, a.shape, mybir.dt.from_np(a.dtype), kind="ExternalInput").ap() for n, a in arrays.items()]
    out = nc.dram_tensor("out_d", (B, S, DM), F32, kind="ExternalOutput").ap()
    build(nc, *aps, out)
    r = run_bass_kernel_spmd(nc, [arrays], core_ids=[0])
    return r.results[0]["out_d"]
```
